# Optimizing a Trainium2 kernel written in Bass

```python
import numpy as np
import jax
import jax.numpy as jnp

def _softmax(x, axis=-1):
    return jax.nn.softmax(x, axis=axis)

def _gelu(x):
    return jax.nn.gelu(x, approximate=True)

def _silu(x):
    return jax.nn.silu(x)

def _sigmoid(x):
    return jax.nn.sigmoid(x)

def _layernorm(x, axis=-1, eps=1e-05):
    m = jnp.mean(x, axis=axis, keepdims=True)
    v = jnp.var(x, axis=axis, keepdims=True)
    return (x - m) / jnp.sqrt(v + eps)

def _scatter_add(tgt, idx, src, axis=0):
    return tgt.at[idx].add(src)

def _segment_sum(src, seg, n):
    return jax.ops.segment_sum(src, seg, n)
kernel_name = 'mk_seq_postln_d1_jaxref_r8_e687d2'

def setup_inputs(seed: int=0):
    np.random.seed(seed)
    _w = jnp.asarray

    def _L0_attn_setup():
        import jax, jax.numpy as jnp
        import numpy as np
        DIM = 128
        HEADS = 16
        HEAD_DIM = DIM // HEADS
        FEAT = 32
        B, N = (4, 512)

        def _elu1(x):
            return jnp.where(x > 0, x + 1.0, jnp.exp(x))
        key = jax.random.key(seed)
        k_x, k_qkv, k_proj, k_wo, k_bo = jax.random.split(key, 5)
        x = jax.random.normal(k_x, (B, N, DIM), dtype=jnp.float32)
        w_qkv = jax.random.normal(k_qkv, (DIM, 3 * DIM), dtype=jnp.float32) * (1.0 / np.sqrt(DIM))
        proj_matrix = jax.random.normal(k_proj, (HEADS, HEAD_DIM, FEAT), dtype=jnp.float32) * (1.0 / np.sqrt(HEAD_DIM))
        w_out = jax.random.normal(k_wo, (DIM, DIM), dtype=jnp.float32) * (1.0 / np.sqrt(DIM))
        b_out = jax.random.normal(k_bo, (DIM,), dtype=jnp.float32) * 0.01
        return {'x': x, 'w_qkv': w_qkv, 'proj_matrix': proj_matrix, 'w_out': w_out, 'b_out': b_out}
    _L0_attn_in = _L0_attn_setup()

    def _L0_ffn_setup():
        import jax, jax.numpy as jnp
        import numpy as np
        B, S, H, F, E = (4, 256, 128, 512, 8)
        key = jax.random.key(seed)
        ks = jax.random.split(key, 8)
        s = 1.0 / np.sqrt(H)
        sf = 1.0 / np.sqrt(F)
        return {'x': jax.random.normal(ks[0], (B, S, H), jnp.float32), 'wr': jax.random.uniform(ks[1], (H, E), jnp.float32, -s, s), 'br': jax.random.uniform(ks[2], (E,), jnp.float32, -s, s), 'w1': jax.random.uniform(ks[3], (E, H, F), jnp.float32, -s, s), 'b1': jax.random.uniform(ks[4], (E, F), jnp.float32, -s, s), 'w2': jax.random.uniform(ks[5], (E, F, H), jnp.float32, -sf, sf), 'b2': jax.random.uniform(ks[6], (E, H), jnp.float32, -sf, sf)}
    _L0_ffn_in = _L0_ffn_setup()
    _d = {'L0_attn_x': _L0_attn_in['x'], 'L0_attn_w_qkv': _L0_attn_in['w_qkv'], 'L0_attn_proj_matrix': _L0_attn_in['proj_matrix'], 'L0_attn_w_out': _L0_attn_in['w_out'], 'L0_attn_b_out': _L0_attn_in['b_out'], 'L0_ffn_wr': _L0_ffn_in['wr'], 'L0_ffn_br': _L0_ffn_in['br'], 'L0_ffn_w1': _L0_ffn_in['w1'], 'L0_ffn_b1': _L0_ffn_in['b1'], 'L0_ffn_w2': _L0_ffn_in['w2'], 'L0_ffn_b2': _L0_ffn_in['b2']}
    _x0 = _d['L0_attn_x']
    _d['L0_attn_x'] = jax.random.normal(jax.random.fold_in(jax.random.key(seed), 1), (4, 1024, 128), dtype=_x0.dtype)
    del _x0
    return _d

def reference(L0_attn_x, L0_attn_w_qkv, L0_attn_proj_matrix, L0_attn_w_out, L0_attn_b_out, L0_ffn_wr, L0_ffn_br, L0_ffn_w1, L0_ffn_b1, L0_ffn_w2, L0_ffn_b2):

    def _L0_attn_ref(x, w_qkv, proj_matrix, w_out, b_out):
        import jax, jax.numpy as jnp
        import numpy as np
        DIM = 128
        HEADS = 16
        HEAD_DIM = DIM // HEADS
        FEAT = 32
        B, N = (4, 512)

        def _elu1(x):
            return jnp.where(x > 0, x + 1.0, jnp.exp(x))
        b, n, d = x.shape
        h, hd = (HEADS, HEAD_DIM)
        qkv = x @ w_qkv
        q, k, v = jnp.split(qkv, 3, axis=-1)
        to_heads = lambda t: t.reshape(b, n, h, hd).transpose(0, 2, 1, 3)
        q, k, v = (to_heads(q), to_heads(k), to_heads(v))
        q_proj = _elu1(jnp.einsum('bhnd,hdf->bhnf', q, proj_matrix))
        k_proj = _elu1(jnp.einsum('bhnd,hdf->bhnf', k, proj_matrix))
        kv = jnp.einsum('bhnf,bhnd->bhfd', k_proj, v)
        attn = jnp.einsum('bhnf,bhfd->bhnd', q_proj, kv)
        k_sum = k_proj.sum(axis=2)
        z = 1.0 / (jnp.einsum('bhnf,bhf->bhn', q_proj, k_sum) + 1e-08)
        attn = attn * z[..., None]
        out = attn.transpose(0, 2, 1, 3).reshape(b, n, d)
        return out @ w_out + b_out

    def _L0_ffn_ref(x, wr, br, w1, b1, w2, b2):
        import jax, jax.numpy as jnp
        import numpy as np
        B, S, H, F, E = (4, 256, 128, 512, 8)
        scores = jnp.einsum('bsh,he->bse', x, wr) + br
        expert_id = jnp.argmax(scores, axis=-1)
        h = jnp.einsum('bsh,ehf->ebsf', x, w1) + b1[:, None, None, :]
        h = jax.nn.gelu(h, approximate=False)
        y = jnp.einsum('ebsf,efh->ebsh', h, w2) + b2[:, None, None, :]
        one_hot = jax.nn.one_hot(expert_id, E, dtype=x.dtype)
        out = jnp.einsum('ebsh,bse->bsh', y, one_hot)
        return out
    x = L0_attn_x
    x = _layernorm(x + _L0_attn_ref(x, L0_attn_w_qkv, L0_attn_proj_matrix, L0_attn_w_out, L0_attn_b_out), axis=-1)
    x = _layernorm(x + _L0_ffn_ref(x, L0_ffn_wr, L0_ffn_br, L0_ffn_w1, L0_ffn_b1, L0_ffn_w2, L0_ffn_b2), axis=-1)
    return x

_drawn_inputs = setup_inputs


def setup_inputs(seed=0):
    import zlib

    import numpy as np

    out = dict(_drawn_inputs(seed))
    spreads = {}
    factors = {'L0_ffn_b1': 3.144}
    for name, (base, spread) in spreads.items():
        noise = np.random.default_rng([zlib.crc32(name.encode()), seed]).standard_normal(out[name].shape)
        drawn = base * np.exp(spread * noise) if base else spread * noise
        out[name] = jnp.asarray(drawn.astype(out[name].dtype))
    for name, factor in factors.items():
        out[name] = (out[name] * factor).astype(out[name].dtype)
    return out
```

```python
from contextlib import ExitStack

import concourse.bass as bass
from concourse import mybir

F32 = mybir.dt.float32
BF16 = mybir.dt.bfloat16
I32 = mybir.dt.int32
U32 = mybir.dt.uint32
ALU = mybir.AluOpType
ACT = mybir.ActivationFunctionType
AX = mybir.AxisListType

P = 128
LN_EPS = 1e-5
DEN_EPS = 1e-8


def build(nc, x, w_qkv, proj, w_out, b_out, wr, br, w1, b1, w2, b2, out):
    B, N, D = x.shape
    H, HD, F = proj.shape
    E, _, FF = w1.shape
    T = B * N // P
    TB = N // P
    GT = 4
    G = T // GT
    NF = H * F
    C = NF // P
    HC = H // C
    VW = HD + 1
    CW = HC * VW
    FC = FF // P
    NT = T + E - 1
    CAP = B * N + P
    RW = D + 4
    NO_TOKEN = 1 << 20
    assert D == P and C * P == NF and GT * P == 512 and FF == 512 and E == 8

    x_rows = x.rearrange("b n d -> (b n) d")
    out_rows = out.rearrange("b n d -> (b n) d")
    x_groups = x_rows.rearrange("(g i p) d -> g p i d", i=GT, p=P)
    sorted_rows = nc.dram_tensor("sorted_rows", [E * CAP, RW], F32, kind="Internal").ap()

    ctx = ExitStack()
    with ctx:
        def sb(name, shape, dt=F32):
            return ctx.enter_context(nc.sbuf_tensor(name, shape, dt))

        def sem(name):
            return ctx.enter_context(nc.semaphore(name))

        bank = [ctx.enter_context(nc.psum_tensor(f"bank{i}", [P, 512], F32)) for i in range(8)]

        ident = sb("ident", [P, P])
        before = sb("before", [P, P], BF16)
        ones_bf = sb("ones_bf", [P, P], BF16)
        head_mask = sb("head_mask", [P, H])
        wqkv_sb = sb("wqkv_sb", [P, 3 * D])
        proj_sb = sb("proj_sb", [P, F])
        proj_diag = sb("proj_diag", [P, H, F])
        wT = sb("wT", [P, 2, P])
        w_feat = sb("w_feat", [P, 2, NF])
        wout_sb = sb("wout_sb", [P, D])
        bout_sb = sb("bout_sb", [P, D])
        wr_sb = sb("wr_sb", [P, E])
        br_sb = sb("br_sb", [P, E])
        w1_sb = sb("w1_sb", [P, E * FF])
        b1_sb = sb("b1_sb", [P, E * FF])
        w2_sb = sb("w2_sb", [P, E * FF])
        b2_sb = sb("b2_sb", [P, E * D])
        minus_half = sb("minus_half", [P, GT])
        expert_no = sb("expert_no", [P, E])
        region = sb("region", [P, E])
        xr = sb("xr", [P, 2, GT, D])
        xT = sb("xT", [P, 2, P])
        xT_all = sb("xT_all", [P, T * P])
        kexp = sb("kexp", [P, 2, NF])
        kfeat = sb("kfeat", [P, 2, NF])
        v_ones = sb("v_ones", [P, 2, H, VW])
        kv_diag = sb("kv_diag", [P, B * C * CW])
        xg = sb("xg", [P, 2, GT, D])
        qexp = sb("qexp", [P, 2, 512])
        qfeat = sb("qfeat", [P, 2, C, 512])
        den = sb("den", [P, GT, H])
        rden = sb("rden", [P, GT, H])
        attn = sb("attn", [P, 2, GT, D])
        attnT = sb("attnT", [P, 2, GT * P])
        res = sb("res", [P, 2, GT, D])
        stats = sb("stats", [P, GT, 6])
        mean_var = sb("mean_var", [P, 2, GT, 2])
        var_eps = sb("var_eps", [P, 2, GT])
        rstd = sb("rstd", [P, 2, GT])
        x1 = sb("x1", [P, 2, GT, RW])
        x1T = sb("x1T", [P, 2, GT * P])
        score = sb("score", [P, GT, E])
        top = sb("top", [P, GT, 8])
        top_at = sb("top_at", [P, GT, 8], U32)
        onehot = sb("onehot", [P, GT + 1, E], BF16)
        next_row = sb("next_row", [P, E])
        row_of = sb("row_of", [P, GT, E])
        row_pick = sb("row_pick", [P, GT, E])
        dest = sb("dest", [P, 2, GT], I32)
        used = sb("used", [1, E])
        used_i = sb("used_i", [1, E], I32)
        tiles_i = sb("tiles_i", [1, E], I32)
        tiles_f = sb("tiles_f", [1, E])
        ones_e = sb("ones_e", [1, E])
        tiles_end = sb("tiles_end", [1, E])
        jump = sb("jump", [1, E])
        tile_no = sb("tile_no", [1, NT])
        past = sb("past", [1, NT, E - 1])
        past_jump = sb("past_jump", [1, NT, E - 1])
        t_expert = sb("t_expert", [1, NT])
        t_jump = sb("t_jump", [1, NT])
        t_row = sb("t_row", [1, NT])
        pad_at = sb("pad_at", [1, E], I32)
        row_tab = sb("row_tab", [1, NT], I32)
        w_tab = sb("w_tab", [1, NT], I32)
        b2_tab = sb("b2_tab", [1, NT], I32)
        pad_rows = sb("pad_rows", [P, RW])
        XS = 4
        xs = sb("xs", [P, XS, RW])
        xsT = sb("xsT", [P, 2, P])
        hid = sb("hid", [P, 2, FF])
        hT = sb("hT", [P, 2, FF])
        xb2 = sb("xb2", [P, XS, RW])
        res3 = sb("res3", [P, 2, D])
        stats3 = sb("stats3", [P, 6])
        mv3 = sb("mv3", [P, 2, 2])
        ve3 = sb("ve3", [P, 2, 1])
        rstd3 = sb("rstd3", [P, 2, 1])
        y = sb("y", [P, 4, D])

        const_in = sem("const_in")
        ffn_in = sem("ffn_in")
        zeroed = sem("zeroed")
        pool_consts = sem("pool_consts")
        w_turned = sem("w_turned")
        w_turn_kept = sem("w_turn_kept")
        proj_ready = sem("proj_ready")
        w_feat_pre = sem("w_feat_pre")
        w_feat_ready = sem("w_feat_ready")
        x_loaded = [sem("x_loaded0"), sem("x_loaded1")]
        x_turned = sem("x_turned")
        xT_ready = sem("xT_ready")
        xT_kept = sem("xT_kept")
        k_pre = sem("k_pre")
        v_pre = sem("v_pre")
        k_exp = sem("k_exp")
        k_min = sem("k_min")
        k_done = sem("k_done")
        v_ready = sem("v_ready")
        kv_added = sem("kv_added")
        kv_kept = sem("kv_kept")

        xg_loaded = [sem("xg_loaded0"), sem("xg_loaded1")]
        xb_done = sem("xb_done")
        q_pre = sem("q_pre")
        q_exp = sem("q_exp")
        q_min = sem("q_min")
        q_done = sem("q_done")
        attn_pre = sem("attn_pre")
        den_ready = sem("den_ready")
        rden_ready = sem("rden_ready")
        attn_ready = sem("attn_ready")
        attn_turned = sem("attn_turned")
        attnT_ready = sem("attnT_ready")
        out_pre = sem("out_pre")
        res_ready = sem("res_ready")
        stats_ready = sem("stats_ready")
        mv_ready = sem("mv_ready")
        ve_ready = sem("ve_ready")
        rstd_ready = sem("rstd_ready")
        number_ready = sem("number_ready")
        x1_ready = sem("x1_ready")
        x1_turned = sem("x1_turned")
        x1T_ready = sem("x1T_ready")
        score_pre = sem("score_pre")
        score_ready = sem("score_ready")
        top_ready = sem("top_ready")
        top_at_ready = sem("top_at_ready")
        onehot_ready = sem("onehot_ready")
        rank_pre = sem("rank_pre")
        row_ready = sem("row_ready")
        pick_ready = sem("pick_ready")
        next_ready = sem("next_ready")
        dest_ready = sem("dest_ready")
        scattered = [sem("scattered0"), sem("scattered1")]

        tab_step = sem("tab_step")
        padded = sem("padded")
        xs_loaded = [sem(f"xs_loaded{i}") for i in range(XS)]
        xs_turned = sem("xs_turned")
        xsT_ready = sem("xsT_ready")
        hid_pre = sem("hid_pre")
        hid_ready = sem("hid_ready")
        hid_turned = sem("hid_turned")
        hT_ready = sem("hT_ready")
        y_pre = sem("y_pre")
        xb2_ready = sem("xb2_ready")
        no_ready = sem("no_ready")
        res3_ready = sem("res3_ready")
        stats3_ready = sem("stats3_ready")
        mv3_ready = sem("mv3_ready")
        ve3_ready = sem("ve3_ready")
        rstd3_ready = sem("rstd3_ready")
        y_ready = sem("y_ready")
        stored = [sem(f"stored{i}") for i in range(4)]

        TAB_STEPS = 16

        def reach(eng, s, count):
            if not isinstance(count, int) or count > 0:
                eng.wait_ge(s, count)

        def skewed(eng, step, n, lead, lag, first, unroll):
            turns = (n - lead - first) // unroll
            for s in range(-lead, first):
                step(0, s)
            with eng.Fori(0, turns, 1) as j:
                for c in range(first, first + unroll):
                    step(j, c)
            for s in range(first + turns * unroll, n + lag):
                step(0, s)

        def exists(j, c, n):
            return not isinstance(j, int) or 0 <= c < n

        LEAD1, LAG1, FIRST1 = 2, 0, 1
        LEAD3, LAG3, FIRST3 = 2, 2, 3
        xT_bank = [bank[0], bank[1]]
        k_bank = [bank[2], bank[3]]
        v_bank = [bank[4], bank[5]]
        kv_bank = bank[6]

        q_bank = [bank[0], bank[1]]
        a_bank = [bank[2], bank[3]]
        t1_bank, o_bank, t2_bank, s_bank = bank[4], bank[5], bank[6], bank[7]

        xs_bank = [bank[0], bank[1]]
        h_bank = [bank[2], bank[3]]
        hT_bank = [bank[4], bank[5]]
        y_bank = [bank[6], bank[7]]

        PASS2 = range(0, G + 3)
        block = ctx.enter_context(nc.Block())

        @block.sync
        def _(sp):
            sp.dma_start(wqkv_sb[:, :], w_qkv).then_inc(const_in, 16)
            sp.dma_start(proj_sb[:, :], proj.rearrange("h d f -> (h d) f")).then_inc(const_in, 16)
            sp.dma_start(xr[:, 0, :, :], x_groups[0]).then_inc(x_loaded[0], 16)
            sp.dma_start(xr[:, 1, :, :], x_groups[1]).then_inc(x_loaded[1], 16)
            sp.dma_start(wout_sb[:, :], w_out).then_inc(const_in, 16)
            sp.dma_start(bout_sb[:, :], b_out.rearrange("(a d) -> a d", a=1).to_broadcast([P, D])).then_inc(const_in, 16)
            sp.dma_start(wr_sb[:, :], wr).then_inc(const_in, 16)
            sp.dma_start(br_sb[:, :], br.rearrange("(a d) -> a d", a=1).to_broadcast([P, E])).then_inc(const_in, 16)
            with sp.Fori(1, G // 2, 1) as j:
                for par in range(2):
                    sp.wait_ge(x_turned, (j * 2 + (par - 1)) * GT)
                    rows = x_rows[bass.ds((j * 2 + par) * (GT * P), GT * P), :]
                    sp.dma_start(xr[:, par, :, :], rows.rearrange("(i p) d -> p i d", p=P)).then_inc(x_loaded[par], 16)
            sp.dma_start(w1_sb[:, :].rearrange("p (e f) -> p e f", e=E), w1.rearrange("e h f -> h e f")).then_inc(ffn_in, 16)
            sp.dma_start(w2_sb[:, :].rearrange("p (e c h) -> p e c h", e=E, c=FC),
                         w2.rearrange("e (c p) h -> p e c h", p=P)).then_inc(ffn_in, 16)
            sp.dma_start(b1_sb[:, :], b1.rearrange("(a e) f -> a (e f)", a=1).to_broadcast([P, E * FF])).then_inc(ffn_in, 16)
            sp.dma_start(b2_sb[:, :], b2.rearrange("(a e) f -> a (e f)", a=1).to_broadcast([P, E * D])).then_inc(ffn_in, 16)
            for g in range(G):
                reach(sp, res_ready, g - 1)
                sp.dma_start(xg[:, g % 2, :, :], x_groups[g]).then_inc(xg_loaded[g % 2], 16)
            sp.wait_ge(tab_step, TAB_STEPS)
            sp.wait_ge(pool_consts, 1)
            for e in range(E):
                at = sp.value_load(pad_at[0:1, e:e + 1], min_val=0, max_val=E * CAP - P)
                sp.dma_start(sorted_rows[bass.ds(at, P), :], pad_rows[:, :]).then_inc(padded, 16)
            sp.wait_ge(padded, 16 * E)
            for par in range(2):
                sp.wait_ge(scattered[par], 16 * GT * G // 2)

            def load(j, c):
                slot = c % XS
                t = j * 4 + c
                reach(sp, xb2_ready, t - XS + 1)
                reach(sp, xs_turned, t - XS + 1)
                reach(sp, no_ready, t - XS + 1)
                at = sp.value_load(row_tab[0:1, bass.ds(t, 1)], min_val=0, max_val=E * CAP - P)
                sp.dma_start(xs[:, slot, :], sorted_rows[bass.ds(at, P), :]).then_inc(xs_loaded[slot], 16)
            for t in range(XS):
                load(0, t)
            with sp.Fori(1, NT // XS, 1) as j:
                for c in range(XS):
                    load(j, c)
            for t in range(NT // XS * XS, NT):
                load(0, t)

        @block.gpsimd
        def _(pool):
            g_ = nc.gpsimd
            g_.memset(ident[:, :], 1.0).then_inc(zeroed, 1)
            g_.memset(before[:, :], 1.0).then_inc(zeroed, 1)
            g_.memset(head_mask[:, :], 1.0).then_inc(zeroed, 1)
            g_.memset(ones_bf[:, :], 1.0)
            g_.memset(v_ones[:, :, :, :], 1.0)
            g_.memset(kv_diag[:, :], 0.0)
            g_.memset(onehot[:, :, :], 0.0)
            g_.memset(minus_half[:, :], -0.5)
            g_.memset(x1[:, :, :, :], 0.0).then_inc(zeroed, 1)
            g_.memset(pad_rows[:, :], 0.0).then_inc(zeroed, 1)
            g_.memset(ones_e[:, :], 1.0)
            pool.wait_ge(zeroed, 5)
            g_.affine_select(out=ident[:, :], in_=ident[:, :], compare_op=ALU.is_equal, fill=0.0, base=0,
                             pattern=[[-1, P]], channel_multiplier=1)
            g_.affine_select(out=before[:, :], in_=before[:, :], compare_op=ALU.is_gt, fill=0.0, base=0,
                             pattern=[[1, P]], channel_multiplier=-1)
            g_.affine_select(out=head_mask[:, :], in_=head_mask[:, :], compare_op=ALU.is_ge, fill=0.0, base=0,
                             pattern=[[-HD, H]], channel_multiplier=1).then_inc(zeroed, 1)
            pool.wait_ge(zeroed, 6)
            g_.affine_select(out=head_mask[:, :], in_=head_mask[:, :], compare_op=ALU.is_ge, fill=0.0, base=HD - 1,
                             pattern=[[HD, H]], channel_multiplier=-1)
            g_.iota(expert_no[:, :], pattern=[[1, E]], base=0, channel_multiplier=0, allow_small_or_imprecise_dtypes=True)
            g_.iota(region[:, :], pattern=[[CAP, E]], base=0, channel_multiplier=0, allow_small_or_imprecise_dtypes=True)
            g_.iota(next_row[:, :], pattern=[[CAP, E]], base=0, channel_multiplier=0, allow_small_or_imprecise_dtypes=True)
            g_.iota(tile_no[:, :], pattern=[[1, NT]], base=0, channel_multiplier=0, allow_small_or_imprecise_dtypes=True)
            g_.iota(pad_rows[:, D:D + 1].bitcast(I32), pattern=[[0, 1]], base=NO_TOKEN, channel_multiplier=0).then_inc(pool_consts, 1)

            def keep(j, c):
                def item(j, c):
                    t = j * TB + c
                    pool.wait_ge(xT_ready, t + 1)
                    g_.tensor_copy(xT_all[:, bass.ds(t * P, P)], xT[:, c % 2, :]).then_inc(xT_kept, 1)
                if exists(j, c + 2, T):
                    item(j, c + 2)
            skewed(pool, keep, T, LEAD1, LAG1, FIRST1, TB)

            def residual_base(g):
                par = g % 2
                if g == 0:
                    pool.wait_ge(const_in, 16 * 6)
                pool.wait_ge(xg_loaded[par], 16 * (g // 2 + 1))
                g_.tensor_tensor(xg[:, par, :, :], xg[:, par, :, :],
                                 bout_sb[:, :].unsqueeze(1).to_broadcast([P, GT, D]), ALU.add).then_inc(xb_done, 1)

            def inverse_deviation(g):
                par = g % 2
                pool.wait_ge(ve_ready, g + 1)
                reach(pool, x1_ready, g - 1)
                g_.tensor_tensor(rstd[:, par, :], var_eps[:, par, :], minus_half[:, :], ALU.pow).then_inc(rstd_ready, 1)

            def token_numbers(g):
                par = g % 2
                if g >= 2:
                    pool.wait_ge(scattered[par], 16 * GT * (g // 2))
                g_.iota(x1[:, par, :, D:D + 1].bitcast(I32), pattern=[[P, GT], [0, 1]], base=g * GT * P,
                        channel_multiplier=1).then_inc(number_ready, 1)

            def scatter(g):
                par = g % 2
                pool.wait_ge(dest_ready, g + 1)
                pool.wait_ge(x1_ready, g + 1)
                pool.wait_ge(number_ready, g + 1)
                for i in range(GT):
                    g_.indirect_dma_start(out=sorted_rows, out_offset=bass.IndirectOffsetOnAxis(ap=dest[:, par, i:i + 1], axis=0),
                                          in_=x1[:, par, i, :], in_offset=None).then_inc(scattered[par], 16)

            for s in PASS2:
                if s < G:
                    residual_base(s)
                if 0 <= s - 3 < G:
                    scatter(s - 3)
                if 0 <= s - 2 < G:
                    token_numbers(s - 2)
                    inverse_deviation(s - 2)

            pool.wait_ge(tab_step, TAB_STEPS)
            pool.wait_ge(ffn_in, 16 * 4)

            last_token = pool.to_reg(B * N - 1)

            def step3(j, c):
                def base(j, c):
                    t, slot = j * 4 + c, c % XS
                    pool.wait_ge(xs_loaded[slot], 16 * (j + c // XS + 1))
                    reach(pool, res3_ready, t - 3)
                    if not isinstance(t, int) or t >= XS:
                        pool.wait_ge(stored[slot], 16 * (j + c // XS))
                    at = pool.value_load(b2_tab[0:1, bass.ds(t, 1)], min_val=0, max_val=(E - 1) * D)
                    g_.tensor_tensor(xb2[:, slot, 0:D], xs[:, slot, 0:D], b2_sb[:, bass.ds(at, D)], ALU.add).then_inc(xb2_ready, 1)
                    g_.tensor_copy(xb2[:, slot, D:D + 1].bitcast(I32), xs[:, slot, D:D + 1].bitcast(I32)).then_inc(no_ready, 1)

                def inverse(j, c):
                    t = j * 4 + c
                    pool.wait_ge(ve3_ready, t + 1)
                    g_.tensor_tensor(rstd3[:, c % 2, :], ve3[:, c % 2, :], minus_half[:, 0:1], ALU.pow).then_inc(rstd3_ready, 1)

                def store(c):
                    slot = c % 4
                    g_.indirect_dma_start(out=out_rows, out_offset=bass.IndirectOffsetOnAxis(ap=xb2[:, slot, D:D + 1].bitcast(I32), axis=0),
                                          in_=y[:, slot, :], in_offset=None, bounds_check=last_token,
                                          oob_is_err=False).then_inc(stored[slot], 16)
                if exists(j, c, NT):
                    base(j, c)
                if exists(j, c - 2, NT):
                    pool.wait_ge(y_ready, j * 4 + (c - 1))
                    pool.wait_ge(no_ready, j * 4 + (c - 1))
                if exists(j, c - 1, NT):
                    inverse(j, c - 1)
                if exists(j, c - 2, NT):
                    store(c - 2)
            skewed(pool, step3, NT, LEAD3, LAG3, FIRST3, 4)
            for i in range(4):
                pool.wait_ge(stored[i], 16 * len(range(i, NT, 4)))

        @block.tensor
        def _(pe):
            mm = nc.tensor.matmul
            pe.wait_ge(pool_consts, 1)
            pe.wait_ge(const_in, 16 * 6)
            for i in range(2):
                nc.tensor.transpose(bank[0][:, i * P:(i + 1) * P], wqkv_sb[:, i * D:(i + 1) * D], ident[:, :]).then_inc(w_turned, 1)
            pe.wait_ge(w_turn_kept, 1)
            pe.wait_ge(proj_ready, 1)
            for i in range(2):
                mm(bank[1 + i][:, :], wT[:, i, :], proj_diag[:, :, :].rearrange("p h f -> p (h f)"),
                   start=True, stop=True).then_inc(w_feat_pre, 1)
            pe.wait_ge(w_feat_ready, 2)

            def step1(j, c):
                def turn(j, c):
                    t, b = j * TB + c, j + c // TB
                    pe.wait_ge(x_loaded[(c // GT) % 2], 16 * (b + 1))
                    reach(pe, xT_ready, t - 1)
                    nc.tensor.transpose(xT_bank[c % 2][:, 0:P], xr[:, (c // GT) % 2, c % GT, :], ident[:, :]).then_inc(x_turned, 1)

                def keys_values(j, c):
                    t = j * TB + c
                    pe.wait_ge(xT_ready, t + 1)
                    reach(pe, k_done, t - 1)
                    mm(k_bank[c % 2][:, :], xT[:, c % 2, :], w_feat[:, 1, :], start=True, stop=True).then_inc(k_pre, 1)
                    reach(pe, v_ready, t - 1)
                    mm(v_bank[c % 2][:, 0:D], xT[:, c % 2, :], wqkv_sb[:, 2 * D:3 * D], start=True, stop=True).then_inc(v_pre, 1)

                def add_kv(j, c):
                    t, b = j * TB + c, j + c // TB
                    pe.wait_ge(k_done, t + 1)
                    pe.wait_ge(v_ready, t + 1)
                    if c % TB == 0:
                        reach(pe, kv_kept, b)
                    for k in range(C):
                        last = mm(kv_bank[:, k * CW:(k + 1) * CW], kfeat[:, c % 2, k * P:(k + 1) * P],
                                  v_ones[:, c % 2, k * HC:(k + 1) * HC, :].rearrange("p h w -> p (h w)"),
                                  start=(c % TB == 0 and k == 0), stop=(c % TB == TB - 1), skip_group_check=True)
                    last.then_inc(kv_added, 1)
                if exists(j, c + 2, T):
                    turn(j, c + 2)
                if exists(j, c + 1, T):
                    keys_values(j, c + 1)
                if exists(j, c, T):
                    add_kv(j, c)
            skewed(pe, step1, T, LEAD1, LAG1, FIRST1, TB)

            def q_chunk(g, k):
                n = g * C + k
                if n == 0:
                    pe.wait_ge(xT_kept, T)
                    pe.wait_ge(xT_ready, T)
                reach(pe, q_done, n - 1)
                mm(q_bank[k % 2][:, :], w_feat[:, 0, k * P:(k + 1) * P], xT_all[:, g * 512:(g + 1) * 512],
                   start=True, stop=True).then_inc(q_pre, 1)

            def attend(g):
                b = g * GT // TB
                pe.wait_ge(q_done, C * (g + 1))
                pe.wait_ge(kv_kept, B)
                reach(pe, attn_ready, g)
                for i in range(GT):
                    for k in range(C):
                        at = (i % 2) * C * CW + k * CW
                        last = mm(a_bank[i // 2][:, at:at + CW], qfeat[:, g % 2, k, i * P:(i + 1) * P],
                                  kv_diag[:, (b * C + k) * CW:(b * C + k + 1) * CW], start=True, stop=True)
                last.then_inc(attn_pre, 1)

            def turn_attn(g):
                pe.wait_ge(attn_ready, g + 1)
                reach(pe, attnT_ready, g)
                for i in range(GT):
                    last = nc.tensor.transpose(t1_bank[:, i * P:(i + 1) * P], attn[:, g % 2, i, :], ident[:, :])
                last.then_inc(attn_turned, 1)

            def project(g):
                pe.wait_ge(attnT_ready, g + 1)
                reach(pe, res_ready, g)
                for i in range(GT):
                    last = mm(o_bank[:, i * P:(i + 1) * P], attnT[:, g % 2, i * P:(i + 1) * P], wout_sb[:, :],
                              start=True, stop=True)
                last.then_inc(out_pre, 1)

            def turn_x1(g):
                pe.wait_ge(x1_ready, g + 1)
                reach(pe, x1T_ready, g)
                for i in range(GT):
                    last = nc.tensor.transpose(t2_bank[:, i * P:(i + 1) * P], x1[:, g % 2, i, 0:D], ident[:, :])
                last.then_inc(x1_turned, 1)

            def scores(g):
                pe.wait_ge(x1T_ready, g + 1)
                reach(pe, next_ready, g)
                for i in range(GT):
                    last = mm(s_bank[:, i * E:(i + 1) * E], x1T[:, g % 2, i * P:(i + 1) * P], wr_sb[:, :],
                              start=True, stop=True)
                last.then_inc(score_pre, 1)

            def ranks(g):
                pe.wait_ge(onehot_ready, g + 1)
                slots = s_bank[:, 64:64 + (GT + 1) * E]
                mm(slots, before[:, :], onehot[:, :, :].rearrange("p i e -> p (i e)"), start=True, stop=False)
                for i in range(GT):
                    last = mm(s_bank[:, 64 + (i + 1) * E:64 + (GT + 1) * E], ones_bf[:, :],
                              onehot[:, i:i + 1, :].to_broadcast([P, GT - i, E]), start=False, stop=(i == GT - 1))
                last.then_inc(rank_pre, 1)

            for s in PASS2:
                if s < G:
                    q_chunk(s, 0)
                if 0 <= s - 3 < G:
                    ranks(s - 3)
                if 0 <= s - 2 < G:
                    project(s - 2)
                if s < G:
                    q_chunk(s, 1)
                if 0 <= s - 1 < G:
                    attend(s - 1)
                if s < G:
                    q_chunk(s, 2)
                if 0 <= s - 2 < G:
                    turn_x1(s - 2)
                if s < G:
                    q_chunk(s, 3)
                if 0 <= s - 2 < G:
                    scores(s - 2)
                if 0 <= s - 1 < G:
                    turn_attn(s - 1)

            pe.wait_ge(tab_step, TAB_STEPS)
            pe.wait_ge(ffn_in, 16 * 4)

            def step3(j, c):
                def turn(j, c):
                    t, slot = j * 4 + c, c % XS
                    pe.wait_ge(xs_loaded[slot], 16 * (j + c // XS + 1))
                    reach(pe, xsT_ready, t - 1)
                    nc.tensor.transpose(xs_bank[c % 2][:, 0:P], xs[:, slot, 0:D], ident[:, :]).then_inc(xs_turned, 1)

                def up(j, c):
                    t = j * 4 + c
                    at = pe.value_load(w_tab[0:1, bass.ds(t, 1)], min_val=0, max_val=(E - 1) * FF)
                    pe.wait_ge(xsT_ready, t + 1)
                    reach(pe, hid_ready, t - 1)
                    mm(h_bank[c % 2][:, :], xsT[:, c % 2, :], w1_sb[:, bass.ds(at, FF)], start=True, stop=True).then_inc(hid_pre, 1)

                def turn_hidden(j, c):
                    t = j * 4 + c
                    pe.wait_ge(hid_ready, t + 1)
                    reach(pe, hT_ready, t - 1)
                    for k in range(FC):
                        last = nc.tensor.transpose(hT_bank[c % 2][:, k * P:(k + 1) * P], hid[:, c % 2, k * P:(k + 1) * P], ident[:, :])
                    last.then_inc(hid_turned, 1)

                def down(j, c):
                    t = j * 4 + c
                    at = pe.value_load(w_tab[0:1, bass.ds(t, 1)], min_val=0, max_val=(E - 1) * FF)
                    pe.wait_ge(hT_ready, t + 1)
                    reach(pe, res3_ready, t - 1)
                    for k in range(FC):
                        last = mm(y_bank[c % 2][:, 0:D], hT[:, c % 2, k * P:(k + 1) * P], w2_sb[:, bass.ds(at + k * D, D)],
                                  start=(k == 0), stop=(k == FC - 1))
                    last.then_inc(y_pre, 1)
                if exists(j, c + 2, NT):
                    turn(j, c + 2)
                if exists(j, c + 1, NT):
                    up(j, c + 1)
                if exists(j, c, NT):
                    turn_hidden(j, c)
                if exists(j, c - 1, NT):
                    down(j, c - 1)
            skewed(pe, step3, NT, LEAD3, LAG3, FIRST3, 4)

        @block.scalar
        def _(act):
            a_ = nc.scalar
            act.wait_ge(w_turned, 2)
            a_.copy(wT[:, :, :].rearrange("p a b -> p (a b)"), bank[0][:, 0:2 * P]).then_inc(w_turn_kept, 1)
            for i in range(2):
                act.wait_ge(w_feat_pre, i + 1)
                a_.copy(w_feat[:, i, :], bank[1 + i][:, :]).then_inc(w_feat_ready, 1)
            act.wait_ge(pool_consts, 1)

            def step1(j, c):
                def keep_xT(j, c):
                    t = j * TB + c
                    act.wait_ge(x_turned, t + 1)
                    reach(act, xT_kept, t - 1)
                    reach(act, v_pre, t - 1)
                    a_.copy(xT[:, c % 2, :], xT_bank[c % 2][:, 0:P]).then_inc(xT_ready, 1)

                def exp_keys(j, c):
                    t = j * TB + c
                    act.wait_ge(k_pre, t + 1)
                    reach(act, k_done, t - 1)
                    a_.activation(kexp[:, c % 2, :], k_bank[c % 2][:, :], ACT.Exp).then_inc(k_exp, 1)

                def values(j, c):
                    t = j * TB + c
                    act.wait_ge(v_pre, t + 1)
                    reach(act, kv_added, t - 1)
                    a_.copy(v_ones[:, c % 2, :, 0:HD], v_bank[c % 2][:, 0:D].rearrange("p (h d) -> p h d", d=HD)).then_inc(v_ready, 1)
                if exists(j, c + 2, T):
                    keep_xT(j, c + 2)
                if exists(j, c + 1, T):
                    exp_keys(j, c + 1)
                    values(j, c + 1)
            skewed(act, step1, T, LEAD1, LAG1, FIRST1, TB)

            def exp_q(g, k):
                n = g * C + k
                act.wait_ge(q_pre, n + 1)
                reach(act, q_done, n - 1)
                a_.activation(qexp[:, k % 2, :], q_bank[k % 2][:, :], ACT.Exp).then_inc(q_exp, 1)

            def keep_attnT(g):
                act.wait_ge(attn_turned, g + 1)
                reach(act, out_pre, g - 1)
                a_.copy(attnT[:, g % 2, :], t1_bank[:, :]).then_inc(attnT_ready, 1)

            def keep_x1T(g):
                act.wait_ge(x1_turned, g + 1)
                reach(act, score_pre, g - 1)
                a_.copy(x1T[:, g % 2, :], t2_bank[:, :]).then_inc(x1T_ready, 1)

            for s in PASS2:
                if s < G:
                    exp_q(s, 0)
                    exp_q(s, 1)
                    exp_q(s, 2)
                if 0 <= s - 2 < G:
                    keep_x1T(s - 2)
                if s < G:
                    exp_q(s, 3)
                if 0 <= s - 1 < G:
                    keep_attnT(s - 1)

            def step3(j, c):
                def keep_xsT(j, c):
                    t = j * 4 + c
                    act.wait_ge(xs_turned, t + 1)
                    reach(act, hid_pre, t - 1)
                    a_.copy(xsT[:, c % 2, :], xs_bank[c % 2][:, 0:P]).then_inc(xsT_ready, 1)

                def gelu(j, c):
                    t = j * 4 + c
                    act.wait_ge(hid_turned, t + 1)
                    reach(act, y_pre, t - 1)
                    a_.activation(hT[:, c % 2, :], hT_bank[c % 2][:, :], ACT.Gelu).then_inc(hT_ready, 1)
                if exists(j, c + 2, NT):
                    keep_xsT(j, c + 2)
                if exists(j, c, NT):
                    gelu(j, c)
            skewed(act, step3, NT, LEAD3, LAG3, FIRST3, 4)

        @block.vector
        def _(dve):
            v = nc.vector
            dve.wait_ge(pool_consts, 1)
            dve.wait_ge(const_in, 16 * 6)
            v.tensor_tensor(proj_diag[:, :, :], proj_sb[:, :].unsqueeze(1).to_broadcast([P, H, F]),
                            head_mask[:, :].unsqueeze(2).to_broadcast([P, H, F]), ALU.mult).then_inc(proj_ready, 1)

            def step1(j, c):
                def features(j, c):
                    t = j * TB + c
                    dve.wait_ge(k_exp, t + 1)
                    v.tensor_scalar(kexp[:, c % 2, :], kexp[:, c % 2, :], 1.0, None, ALU.min).then_inc(k_min, 1)
                    reach(dve, kv_added, t - 1)
                    dve.wait_ge(k_min, t + 1)
                    v.scalar_tensor_tensor(kfeat[:, c % 2, :], k_bank[c % 2][:, :], 1.0, kexp[:, c % 2, :],
                                           ALU.add, ALU.max).then_inc(k_done, 1)

                def keep_kv(j, c):
                    b = j + c // TB
                    dve.wait_ge(kv_added, (b + 1) * TB)
                    for h in range(HC):
                        rows = slice(h * P // HC, (h + 1) * P // HC)
                        dst = kv_diag[rows, bass.ds(b * (C * CW), C * CW)].rearrange("p (c w) -> p c w", c=C)
                        last = v.tensor_copy(dst[:, :, h * VW:(h + 1) * VW],
                                             kv_bank[rows, 0:C * CW].rearrange("p (c w) -> p c w", c=C)[:, :, h * VW:(h + 1) * VW])
                    last.then_inc(kv_kept, 1)
                if exists(j, c + 1, T):
                    features(j, c + 1)
                if exists(j, c, T) and c % TB == TB - 1:
                    keep_kv(j, c)
            skewed(dve, step1, T, LEAD1, LAG1, FIRST1, TB)

            def q_features(g, k):
                n = g * C + k
                dve.wait_ge(q_exp, n + 1)
                v.tensor_scalar(qexp[:, k % 2, :], qexp[:, k % 2, :], 1.0, None, ALU.min).then_inc(q_min, 1)
                reach(dve, attn_pre, g - 1)
                dve.wait_ge(q_min, n + 1)
                v.scalar_tensor_tensor(qfeat[:, g % 2, k, :], q_bank[k % 2][:, :], 1.0, qexp[:, k % 2, :],
                                       ALU.add, ALU.max).then_inc(q_done, 1)

            def normalise_attn(g):
                dve.wait_ge(attn_pre, g + 1)
                half = [a_bank[i][:, 0:2 * C * CW].rearrange("p (a h w) -> p a h w", a=2, w=VW) for i in range(2)]
                for i in range(2):
                    last = v.tensor_scalar(den[:, 2 * i:2 * i + 2, :], half[i][:, :, :, HD], DEN_EPS, None, ALU.add)
                last.then_inc(den_ready, 1)
                dve.wait_ge(den_ready, g + 1)
                v.reciprocal(rden[:, :, :], den[:, :, :]).then_inc(rden_ready, 1)
                dve.wait_ge(rden_ready, g + 1)
                reach(dve, attn_turned, g - 1)
                for i in range(2):
                    last = v.tensor_tensor(attn[:, g % 2, 2 * i:2 * i + 2, :].rearrange("p a (h d) -> p (a h) d", d=HD),
                                           half[i][:, :, :, 0:HD].rearrange("p a h d -> p (a h) d"),
                                           rden[:, 2 * i:2 * i + 2, :].rearrange("p a h -> p (a h)").unsqueeze(2).to_broadcast([P, 2 * H, HD]),
                                           ALU.mult)
                last.then_inc(attn_ready, 1)

            def residual(g):
                par = g % 2
                dve.wait_ge(out_pre, g + 1)
                dve.wait_ge(xb_done, g + 1)
                v.tensor_tensor(res[:, par, :, :], o_bank[:, :].rearrange("p (i d) -> p i d", i=GT), xg[:, par, :, :],
                                ALU.add).then_inc(res_ready, 1)
                dve.wait_ge(res_ready, g + 1)
                for i in range(GT):
                    last = v.bn_stats(stats[:, i, :], res[:, par, i, :])
                last.then_inc(stats_ready, 1)
                dve.wait_ge(stats_ready, g + 1)
                for i in range(GT):
                    last = v.bn_aggr(mean_var[:, par, i, :], stats[:, i, :])
                last.then_inc(mv_ready, 1)
                dve.wait_ge(mv_ready, g + 1)
                v.tensor_scalar(var_eps[:, par, :], mean_var[:, par, :, 1], LN_EPS, None, ALU.add).then_inc(ve_ready, 1)

            def layer_norm(g):
                par = g % 2
                dve.wait_ge(rstd_ready, g + 1)
                dve.wait_ge(number_ready, g + 1)
                for i in range(GT):
                    last = v.tensor_scalar(x1[:, par, i, 0:D], res[:, par, i, :], mean_var[:, par, i, 0:1],
                                           rstd[:, par, i:i + 1], ALU.subtract, ALU.mult)
                last.then_inc(x1_ready, 1)

            def route(g):
                dve.wait_ge(score_pre, g + 1)
                v.tensor_tensor(score[:, :, :], s_bank[:, 0:GT * E].rearrange("p (i e) -> p i e", e=E),
                                br_sb[:, :].unsqueeze(1).to_broadcast([P, GT, E]), ALU.add).then_inc(score_ready, 1)
                dve.wait_ge(score_ready, g + 1)
                for i in range(GT):
                    last = v.max(top[:, i, :], score[:, i, :])
                last.then_inc(top_ready, 1)
                dve.wait_ge(top_ready, g + 1)
                for i in range(GT):
                    last = v.max_index(top_at[:, i, :], top[:, i, :], score[:, i, :])
                last.then_inc(top_at_ready, 1)
                dve.wait_ge(top_at_ready, g + 1)
                v.tensor_tensor(onehot[:, 0:GT, :], expert_no[:, :].unsqueeze(1).to_broadcast([P, GT, E]),
                                top_at[:, :, 0:1].to_broadcast([P, GT, E]), ALU.is_equal).then_inc(onehot_ready, 1)

            def rows(g):
                par = g % 2
                dve.wait_ge(rank_pre, g + 1)
                if g:
                    dve.wait_ge(next_ready, g)
                slots = s_bank[:, 64:64 + (GT + 1) * E].rearrange("p (i e) -> p i e", e=E)
                v.tensor_tensor(row_of[:, :, :], slots[:, 0:GT, :], next_row[:, :].unsqueeze(1).to_broadcast([P, GT, E]),
                                ALU.add).then_inc(row_ready, 1)
                dve.wait_ge(row_ready, g + 1)
                v.tensor_tensor(next_row[:, :], slots[:, GT, :], next_row[:, :], ALU.add).then_inc(next_ready, 1)
                v.tensor_tensor(row_pick[:, :, :], row_of[:, :, :], onehot[:, 0:GT, :], ALU.mult).then_inc(pick_ready, 1)
                dve.wait_ge(pick_ready, g + 1)
                if g >= 2:
                    dve.wait_ge(scattered[par], 16 * GT * (g // 2))
                with nc.allow_low_precision(reason="row numbers are exact integers"):
                    v.tensor_reduce(dest[:, par, :], row_pick[:, :, :], AX.X, ALU.add).then_inc(dest_ready, 1)

            for s in PASS2:
                if s < G:
                    q_features(s, 0)
                if 0 <= s - 3 < G:
                    rows(s - 3)
                if 0 <= s - 2 < G:
                    residual(s - 2)
                if s < G:
                    q_features(s, 1)
                if 0 <= s - 2 < G:
                    layer_norm(s - 2)
                if 0 <= s - 1 < G:
                    normalise_attn(s - 1)
                if s < G:
                    q_features(s, 2)
                    q_features(s, 3)
                if 0 <= s - 2 < G:
                    route(s - 2)

            done = [0]

            def then(ins):
                done[0] += 1
                ins.then_inc(tab_step, 1)
                dve.wait_ge(tab_step, done[0])
            dve.wait_ge(next_ready, G)
            then(v.tensor_copy(pad_at[:, :], next_row[0:1, :]))
            then(v.tensor_tensor(used[:, :], next_row[0:1, :], region[0:1, :], ALU.subtract))
            then(v.tensor_scalar(used_i[:, :], used[:, :], float(P - 1), None, ALU.add))
            then(v.tensor_scalar(tiles_i[:, :], used_i[:, :], P.bit_length() - 1, None, ALU.arith_shift_right))
            then(v.tensor_copy(tiles_f[:, :], tiles_i[:, :]))
            then(v.tensor_tensor_scan(tiles_end[:, :], ones_e[:, :], tiles_f[:, :], 0.0, ALU.mult, ALU.add))
            then(v.tensor_scalar(jump[:, :], tiles_f[:, :], -float(P), float(CAP), ALU.mult, ALU.add))
            then(v.tensor_tensor(past[:, :, :], tile_no[:, :].unsqueeze(2).to_broadcast([1, NT, E - 1]),
                                 tiles_end[:, 0:E - 1].unsqueeze(1).to_broadcast([1, NT, E - 1]), ALU.is_ge))
            then(v.tensor_reduce(t_expert[:, :], past[:, :, :], AX.X, ALU.add))
            then(v.tensor_tensor(past_jump[:, :, :], past[:, :, :],
                                 jump[:, 0:E - 1].unsqueeze(1).to_broadcast([1, NT, E - 1]), ALU.mult))
            then(v.tensor_reduce(t_jump[:, :], past_jump[:, :, :], AX.X, ALU.add))
            then(v.scalar_tensor_tensor(t_row[:, :], tile_no[:, :], float(P), t_jump[:, :], ALU.mult, ALU.add))
            then(v.tensor_scalar(row_tab[:, :], t_row[:, :], next_row[0:1, E - 1:E], None, ALU.min))
            then(v.tensor_scalar(w_tab[:, :], t_expert[:, :], float(FF), None, ALU.mult))
            then(v.tensor_scalar(b2_tab[:, :], t_expert[:, :], float(D), None, ALU.mult))
            then(v.tensor_copy(t_jump[:, :], t_row[:, :]))
            assert done[0] == TAB_STEPS
            dve.wait_ge(ffn_in, 16 * 4)

            def step3(j, c):
                def bias(j, c):
                    t = j * 4 + c
                    at = dve.value_load(w_tab[0:1, bass.ds(t, 1)], min_val=0, max_val=(E - 1) * FF)
                    dve.wait_ge(hid_pre, t + 1)
                    reach(dve, hid_turned, t - 1)
                    v.tensor_tensor(hid[:, c % 2, :], h_bank[c % 2][:, :], b1_sb[:, bass.ds(at, FF)], ALU.add).then_inc(hid_ready, 1)

                def residual3(j, c):
                    t, slot, par = j * 4 + c, c % XS, c % 2
                    dve.wait_ge(y_pre, t + 1)
                    dve.wait_ge(xb2_ready, t + 1)
                    v.tensor_tensor(res3[:, par, :], y_bank[par][:, 0:D], xb2[:, slot, 0:D], ALU.add).then_inc(res3_ready, 1)
                    dve.wait_ge(res3_ready, t + 1)
                    v.bn_stats(stats3[:, :], res3[:, par, :]).then_inc(stats3_ready, 1)
                    dve.wait_ge(pool_consts, 1)
                    dve.wait_ge(stats3_ready, t + 1)
                    v.bn_aggr(mv3[:, par, :], stats3[:, :]).then_inc(mv3_ready, 1)
                    dve.wait_ge(mv3_ready, t + 1)
                    v.tensor_scalar(ve3[:, par, :], mv3[:, par, 1:2], LN_EPS, None, ALU.add).then_inc(ve3_ready, 1)

                def norm3(j, c):
                    t, slot, par = j * 4 + c, c % XS, c % 2
                    dve.wait_ge(rstd3_ready, t + 1)
                    if not isinstance(t, int) or t >= 4:
                        dve.wait_ge(stored[slot], 16 * (j + c // 4))
                    v.tensor_scalar(y[:, slot, :], res3[:, par, :], mv3[:, par, 0:1], rstd3[:, par, 0:1],
                                    ALU.subtract, ALU.mult).then_inc(y_ready, 1)
                if exists(j, c + 1, NT):
                    bias(j, c + 1)
                if exists(j, c - 2, NT):
                    norm3(j, c - 2)
                if exists(j, c - 1, NT):
                    residual3(j, c - 1)
            skewed(dve, step3, NT, LEAD3, LAG3, FIRST3, 4)


_INS = ['L0_attn_x', 'L0_attn_w_qkv', 'L0_attn_proj_matrix', 'L0_attn_w_out', 'L0_attn_b_out', 'L0_ffn_wr',
        'L0_ffn_br', 'L0_ffn_w1', 'L0_ffn_b1', 'L0_ffn_w2', 'L0_ffn_b2']
_OUTS = [((4, 1024, 128), 'float32')]


def kernel(**inputs):
    import numpy as _np
    import concourse.bacc as _bacc
    from concourse import mybir as _mybir
    from concourse.bass_utils import run_bass_kernel_spmd as _run

    nc = _bacc.Bacc("TRN2", target_bir_lowering=False, num_devices=1)
    arrays, args = {}, []
    for name in _INS:
        a = _np.ascontiguousarray(inputs[name])
        arrays[f"in_{name}_dram"] = a
        args.append(nc.dram_tensor(f"in_{name}_dram", a.shape, _mybir.dt.from_np(a.dtype), kind="ExternalInput").ap())
    for i, (shape, dtype) in enumerate(_OUTS):
        dt = _mybir.dt.from_np(_np.dtype(dtype))
        args.append(nc.dram_tensor(f"out_{i}_dram", shape, dt, kind="ExternalOutput").ap())
    build(nc, *args)
    r = _run(nc, [arrays], core_ids=[0])
    got = tuple(r.results[0][f"out_{i}_dram"] for i in range(len(_OUTS)))
    return got[0]
```

```python
from contextlib import ExitStack

import concourse.bass as bass
from concourse import mybir

F32 = mybir.dt.float32
F32R = mybir.dt.float32r
BF16 = mybir.dt.bfloat16
I32 = mybir.dt.int32
U32 = mybir.dt.uint32
ALU = mybir.AluOpType
ACT = mybir.ActivationFunctionType
AX = mybir.AxisListType
ENG = mybir.EngineType

P = 128
LN_EPS = 1e-5
DEN_EPS = 1e-8


def build(nc, x, w_qkv, proj, w_out, b_out, wr, br, w1, b1, w2, b2, out):
    B, N, D = x.shape
    H, HD, F = proj.shape
    E, _, FF = w1.shape
    T = B * N // P
    TB = N // P
    GT = 4
    G = T // GT
    NF = H * F
    C = NF // P
    HC = H // C
    CD = HC * HD
    FC = FF // P
    NT = T + E - 1
    CAP = B * N + P
    RW = D + 4
    NO_TOKEN = 1 << 20
    assert D == P and C * P == NF and GT * P == 512 and FF == 512 and E == 8

    x_rows = x.rearrange("b n d -> (b n) d")
    out_rows = out.rearrange("b n d -> (b n) d")
    x_groups = x_rows.rearrange("(g i p) d -> g p i d", i=GT, p=P)
    sorted_rows = nc.dram_tensor("sorted_rows", [E * CAP, RW], F32, kind="Internal").ap()

    ctx = ExitStack()
    with ctx:
        def sb(name, shape, dt=F32):
            return ctx.enter_context(nc.sbuf_tensor(name, shape, dt))

        def sem(name):
            return ctx.enter_context(nc.semaphore(name))

        pair = [ctx.enter_context(nc.psum_tensor(f"pair{i}", [P, 1024], F32)) for i in range(3)]
        bank = [pair[i // 2][:, (i % 2) * 512:(i % 2 + 1) * 512] for i in range(6)]
        bank += [ctx.enter_context(nc.psum_tensor(f"bank{i}", [P, 512], F32)) for i in range(6, 8)]
        ident = sb("ident", [P, P])
        before = sb("before", [P, P], BF16)
        ones_bf = sb("ones_bf", [P, P], BF16)
        head_mask = sb("head_mask", [P, H])
        wqkv_sb = sb("wqkv_sb", [P, 3 * D])
        proj_sb = sb("proj_sb", [P, F])
        proj_diag = sb("proj_diag", [P, H, F])
        wT = sb("wT", [P, 2, P])
        wq_part = sb("wq_part", [P, 2, NF], F32R)
        wkv_part = sb("wkv_part", [P, 2, NF + D], F32R)
        block_mask = sb("block_mask", [P, 2 * D])
        ones_kv = sb("ones_kv", [P, CD])
        den_eps = sb("den_eps", [P, 1])
        zero = sb("zero", [P, 1])
        wout_sb = sb("wout_sb", [P, D])
        bout_sb = sb("bout_sb", [P, D])
        wr_sb = sb("wr_sb", [P, E])
        br_sb = sb("br_sb", [P, E])
        w1_raw = sb("w1_raw", [P, 2, FF])
        w1_part = sb("w1_part", [P, 2, E * FF], F32R)
        w2_sb = sb("w2_sb", [P, E * FF])
        b12_sb = sb("b12_sb", [P, E * (FF + D)])
        minus_half = sb("minus_half", [P, GT])
        expert_no = sb("expert_no", [P, E])
        region = sb("region", [P, E])
        VB = 4
        xr = sb("xr", [P, 2, GT, D])
        xT_all = sb("xT_all", [P, 2, T * P], F32R)
        kfeat = sb("kfeat", [P, 2, NF])
        vals = sb("vals", [P, VB, D])
        kvT = sb("kvT", [P, 2 * D])
        kv_diag = sb("kv_diag", [P, B * 2 * D])
        QB = 3
        XR = 4
        xg = sb("xg", [P, 2, GT, D])
        qexp = sb("qexp", [P, QB, 512])
        qfeat = sb("qfeat", [P, 2, C, 512])
        den_inv = sb("den_inv", [P, 2, 512])
        newton = sb("newton", [P, 512])
        attnT = sb("attnT", [P, 2, GT * P])
        res = sb("res", [P, 2, GT, D])
        stats = sb("stats", [P, GT, 6])
        mean_var = sb("mean_var", [P, 2, GT, 2])
        var_eps = sb("var_eps", [P, 2, GT])
        rstd = sb("rstd", [P, 2, GT])
        shift = sb("shift", [P, 2, GT])
        x1 = sb("x1", [P, XR, GT, RW])
        x1T = sb("x1T", [P, 2, GT * P])
        score = sb("score", [P, GT, E])
        top = sb("top", [P, GT, 8])
        top_at = sb("top_at", [P, GT, 8], U32)
        onehot = sb("onehot", [P, GT + 1, E], BF16)
        next_row = sb("next_row", [P, E])
        row_of = sb("row_of", [P, GT, E])
        row_pick = sb("row_pick", [P, GT, E])
        dest = sb("dest", [P, XR, GT], I32)
        used = sb("used", [1, E])
        used_i = sb("used_i", [1, E], I32)
        tiles_i = sb("tiles_i", [1, E], I32)
        tiles_f = sb("tiles_f", [1, E])
        ones_e = sb("ones_e", [1, E])
        first_tiles = sb("first_tiles", [1, E])
        left = sb("left", [1, E])
        kept = sb("kept", [1, E - 1])
        base = sb("base", [1, 1])
        tiles_end = sb("tiles_end", [1, E + 1])
        jump = sb("jump", [1, E - 1])
        tile_no = sb("tile_no", [1, NT])
        past = sb("past", [1, NT, E - 1])
        past_jump = sb("past_jump", [1, NT, E - 1])
        t_expert = sb("t_expert", [1, NT])
        t_jump = sb("t_jump", [1, NT])
        t_row = sb("t_row", [1, NT])
        pad_at = sb("pad_at", [1, E], I32)
        row_tab = sb("row_tab", [1, NT], I32)
        w_tab = sb("w_tab", [1, NT], I32)
        b_tab = sb("b_tab", [1, NT], I32)
        pad_rows = sb("pad_rows", [P, RW])
        XS = 12
        NY = 4
        xs = sb("xs", [P, XS, RW])
        xsT = sb("xsT", [P, 2, 2, P], F32R)
        res3 = sb("res3", [P, 2, D])
        stats3 = sb("stats3", [P, 6])
        mv3 = sb("mv3", [P, 2, 2])
        ve3 = sb("ve3", [P, 2, 1])
        rstd3 = sb("rstd3", [P, 2, 1])
        shift3 = sb("shift3", [P, 2, 1])
        yx = sb("yx", [P, 2, D])
        y = sb("y", [P, NY, D])

        const_in = sem("const_in")
        w1_loaded = [sem("w1_loaded0"), sem("w1_loaded1")]
        w1_high = sem("w1_high")
        w1_ready = sem("w1_ready")
        ffn_in = sem("ffn_in")
        zeroed = sem("zeroed")
        pool_consts = sem("pool_consts")
        w_turned = sem("w_turned")
        w_turn_kept = sem("w_turn_kept")
        proj_ready = sem("proj_ready")
        w_feat_pre = sem("w_feat_pre")
        w_high = sem("w_high")
        w_low = sem("w_low")
        x_loaded = [sem("x_loaded0"), sem("x_loaded1")]
        x_turned = sem("x_turned")
        xT_high = sem("xT_high")
        xT_low = sem("xT_low")
        kv_pre = sem("kv_pre")
        k_exp = sem("k_exp")
        k_min = sem("k_min")
        k_neg = sem("k_neg")
        k_done = sem("k_done")
        v_ready = sem("v_ready")
        kv_added = sem("kv_added")
        kvT_kept = sem("kvT_kept")
        kvT_turned = sem("kvT_turned")
        kv_kept = sem("kv_kept")

        xg_loaded = [sem("xg_loaded0"), sem("xg_loaded1")]
        xb_done = sem("xb_done")
        q_pre = sem("q_pre")
        q_exp = sem("q_exp")
        q_min = sem("q_min")
        q_done = sem("q_done")
        q_neg = sem("q_neg")
        attn_pre = sem("attn_pre")
        log_ready = sem("log_ready")
        inv_ready = sem("inv_ready")
        newton_ready = sem("newton_ready")
        rden_ready = sem("rden_ready")
        attnT_ready = sem("attnT_ready")
        out_pre = sem("out_pre")
        res_ready = sem("res_ready")
        stats_ready = sem("stats_ready")
        mv_ready = sem("mv_ready")
        ve_ready = sem("ve_ready")
        rstd_ready = sem("rstd_ready")
        shift_ready = sem("shift_ready")
        number_ready = sem("number_ready")
        x1_ready = sem("x1_ready")
        x1_turned = sem("x1_turned")
        x1T_ready = sem("x1T_ready")
        score_pre = sem("score_pre")
        score_ready = sem("score_ready")
        top_ready = sem("top_ready")
        top_at_ready = sem("top_at_ready")
        onehot_ready = sem("onehot_ready")
        rank_pre = sem("rank_pre")
        row_ready = sem("row_ready")
        pick_ready = sem("pick_ready")
        next_ready = sem("next_ready")
        dest_ready = sem("dest_ready")
        scattered = [sem(f"scattered{i}") for i in range(XR)]

        tab_step = sem("tab_step")
        padded = sem("padded")
        xs_loaded = [sem(f"xs_loaded{i}") for i in range(XS)]
        xs_turned = sem("xs_turned")
        xsT_high = sem("xsT_high")
        xsT_low = sem("xsT_low")
        hid_pre = sem("hid_pre")
        hid_ready = sem("hid_ready")
        hid_turned = sem("hid_turned")
        hT_ready = sem("hT_ready")
        y_pre = sem("y_pre")
        yx_ready = sem("yx_ready")
        shift3_ready = sem("shift3_ready")
        res3_ready = sem("res3_ready")
        stats3_ready = sem("stats3_ready")
        mv3_ready = sem("mv3_ready")
        ve3_ready = sem("ve3_ready")
        rstd3_ready = sem("rstd3_ready")
        y_ready = sem("y_ready")
        stored = [sem(f"stored{i}") for i in range(NY)]

        TAB_A, TAB_B = 16, 18

        def reach(eng, s, count):
            if not isinstance(count, int) or count > 0:
                eng.wait_ge(s, count)

        def offset(eng, kind, table, t, most):
            if t == 0:
                eng.wait_ge(tab_step, TAB_A)
            if t == NA:
                eng.wait_ge(tab_step, TAB_A + TAB_B)
            return nc.values_load(table[0:1, t:t + 1], engines=(kind,), min_val=0, max_val=most,
                                  skip_runtime_bounds_check_because="made on the chip from counts that add up")

        def product(out, weights, moving, spans, stop=True):
            for w, m in ((0, 0), (0, 1), (1, 0)):
                for to, of in spans:
                    last = nc.tensor.matmul(out[:, to], weights[:, w, :], moving[:, m, of], start=(w + m == 0), stop=(w == 1))
            return last

        HALF = NF // 2
        kv_spans = [(slice(0, HALF), slice(0, HALF)), (slice(512, 512 + HALF + D), slice(HALF, NF + D))]
        keys = [pair[i][:, :].rearrange("p (a f) -> p a f", a=2)[:, :, 0:HALF] for i in range(3)]
        values = [pair[i][:, 512 + HALF:512 + HALF + D] for i in range(3)]
        kvT_part = [pair[i][:, HALF:512] for i in range(3)]
        kv_bank, xT_bank = bank[6], bank[7]

        def kvT_pair(b):
            return ((b + 1) * TB + 4) % 3 if b < B - 1 else 2

        kexp = qexp
        hid, hT = qfeat[:, 0, 0:2, :], qfeat[:, 0, 2:4, :]

        q_bank = [bank[0], bank[1], bank[2]]
        num_bank, den_bank = bank[3], bank[4]
        o_bank, t2_bank, s_bank = bank[5], bank[6], bank[7]
        BY_RELU = (0, 2)

        xs_bank, h_bank, hT_bank, y_bank = bank[0], [bank[1], bank[2]], bank[3], bank[4]

        GA = 5
        NA = -((E * (P - 1) - GA * GT * P) // P)
        TILE_STEPS_AFTER = {G + 1: 4, G + 2: 4}
        ORDER, t = [], -2
        for s in range(G + 4):
            ORDER.append(("group", s))
            for _ in range(TILE_STEPS_AFTER.get(s, 0)):
                ORDER.append(("tile", t))
                t += 1
        ORDER += [("tile", i) for i in range(t, NT + 2)]
        MORE_TABLES = range(t, t + 3)
        assert 0 < NA < NT and t + 4 < NA
        block = ctx.enter_context(nc.Block())

        @block.sync
        def _(sp):
            sp.dma_start(wqkv_sb[:, :], w_qkv).then_inc(const_in, 16)
            sp.dma_start(proj_sb[:, :], proj.rearrange("h d f -> (h d) f")).then_inc(const_in, 16)
            sp.dma_start(xr[:, 0, :, :], x_groups[0]).then_inc(x_loaded[0], 16)
            sp.dma_start(xr[:, 1, :, :], x_groups[1]).then_inc(x_loaded[1], 16)
            sp.dma_start(wout_sb[:, :], w_out).then_inc(const_in, 16)
            sp.dma_start(bout_sb[:, :], b_out.rearrange("(a d) -> a d", a=1).to_broadcast([P, D])).then_inc(const_in, 16)
            sp.dma_start(wr_sb[:, :], wr).then_inc(const_in, 16)
            sp.dma_start(br_sb[:, :], br.rearrange("(a d) -> a d", a=1).to_broadcast([P, E])).then_inc(const_in, 16)
            w1_rows = w1.rearrange("e h f -> (e h) f")
            for i in range(2, max(G, E + 2)):
                if i < G:
                    sp.wait_ge(x_turned, (i - 1) * GT)
                    sp.dma_start(xr[:, i % 2, :, :], x_groups[i]).then_inc(x_loaded[i % 2], 16)
                if i - 2 < E:
                    e = i - 2
                    reach(sp, w1_ready, e - 1)
                    sp.dma_start(w1_raw[:, e % 2, :], w1_rows[e * P:(e + 1) * P, :]).then_inc(w1_loaded[e % 2], 16)
            sp.dma_start(w2_sb[:, :].rearrange("p (e c h) -> p e c h", e=E, c=FC),
                         w2.rearrange("e (c p) h -> p e c h", p=P)).then_inc(ffn_in, 16)
            b12 = b12_sb[:, :].rearrange("p (e f) -> p e f", e=E)
            sp.dma_start(b12[:, :, 0:FF], b1.unsqueeze(0).to_broadcast([P, E, FF])).then_inc(ffn_in, 16)
            sp.dma_start(b12[:, :, FF:FF + D], b2.unsqueeze(0).to_broadcast([P, E, D])).then_inc(ffn_in, 16)
            for g in range(G):
                reach(sp, res_ready, g - 1)
                sp.dma_start(xg[:, g % 2, :, :], x_groups[g]).then_inc(xg_loaded[g % 2], 16)
            def load_rows(t):
                reach(sp, xs_turned, t - XS + 1)
                if t >= XS:
                    sp.wait_ge(stored[t % NY], 16 * ((t - XS) // NY + 1))
                at = offset(sp, ENG.SP, row_tab, t, E * CAP - P)
                sp.dma_start(xs[:, t % XS, :], sorted_rows[bass.ds(at, P), :]).then_inc(xs_loaded[t % XS], 16)

            for i in range(XR):
                sp.wait_ge(scattered[i], 16 * GT * len(range(i, GA, XR)))
            for t in range(NA):
                load_rows(t)
            sp.wait_ge(tab_step, TAB_A + 1)
            sp.wait_ge(pool_consts, 1)
            for e in range(E):
                at = sp.value_load(pad_at[0:1, e:e + 1], min_val=0, max_val=E * CAP - P)
                sp.dma_start(sorted_rows[bass.ds(at, P), :], pad_rows[:, :]).then_inc(padded, 16)
            sp.wait_ge(padded, 16 * E)
            for i in range(XR):
                sp.wait_ge(scattered[i], 16 * GT * G // XR)
            for t in range(NA, NT):
                load_rows(t)

        @block.gpsimd
        def _(pool):
            g_ = nc.gpsimd
            g_.memset(ident[:, :], 1.0).then_inc(zeroed, 1)
            g_.memset(before[:, :], 1.0).then_inc(zeroed, 1)
            g_.memset(head_mask[:, :], 1.0).then_inc(zeroed, 1)
            g_.memset(ones_bf[:, :], 1.0)
            g_.memset(ones_kv[:, :], 1.0)
            g_.memset(den_eps[:, :], DEN_EPS)
            g_.memset(zero[:, :], 0.0)
            g_.memset(block_mask[:, :], 1.0).then_inc(zeroed, 1)
            g_.memset(onehot[:, :, :], 0.0)
            g_.memset(minus_half[:, :], -0.5)
            g_.memset(x1[:, :, :, :], 0.0).then_inc(zeroed, 1)
            g_.memset(pad_rows[:, :], 0.0).then_inc(zeroed, 1)
            g_.memset(ones_e[:, :], 1.0)
            g_.memset(tiles_end[:, :], 0.0)
            pool.wait_ge(zeroed, 6)
            g_.affine_select(out=ident[:, :], in_=ident[:, :], compare_op=ALU.is_equal, fill=0.0, base=0,
                             pattern=[[-1, P]], channel_multiplier=1)
            g_.affine_select(out=before[:, :], in_=before[:, :], compare_op=ALU.is_gt, fill=0.0, base=0,
                             pattern=[[1, P]], channel_multiplier=-1)
            g_.affine_select(out=head_mask[:, :], in_=head_mask[:, :], compare_op=ALU.is_ge, fill=0.0, base=0,
                             pattern=[[-HD, H]], channel_multiplier=1).then_inc(zeroed, 1)
            g_.affine_select(out=block_mask[:, :], in_=block_mask[:, :], compare_op=ALU.is_ge, fill=0.0, base=0,
                             pattern=[[0, 2 * C], [-F, HC], [0, HD]], channel_multiplier=1).then_inc(zeroed, 1)
            pool.wait_ge(zeroed, 8)
            g_.affine_select(out=head_mask[:, :], in_=head_mask[:, :], compare_op=ALU.is_ge, fill=0.0, base=HD - 1,
                             pattern=[[HD, H]], channel_multiplier=-1)
            g_.affine_select(out=block_mask[:, :], in_=block_mask[:, :], compare_op=ALU.is_ge, fill=0.0, base=F - 1,
                             pattern=[[0, 2 * C], [F, HC], [0, HD]], channel_multiplier=-1)
            g_.iota(expert_no[:, :], pattern=[[1, E]], base=0, channel_multiplier=0, allow_small_or_imprecise_dtypes=True)
            g_.iota(region[:, :], pattern=[[CAP, E]], base=0, channel_multiplier=0, allow_small_or_imprecise_dtypes=True)
            g_.iota(next_row[:, :], pattern=[[CAP, E]], base=0, channel_multiplier=0, allow_small_or_imprecise_dtypes=True)
            g_.iota(tile_no[:, :], pattern=[[1, NT]], base=0, channel_multiplier=0, allow_small_or_imprecise_dtypes=True)
            g_.iota(pad_rows[:, D:D + 1].bitcast(I32), pattern=[[0, 1]], base=NO_TOKEN, channel_multiplier=0).then_inc(pool_consts, 1)

            for e in range(E):
                units = slice(e * FF, (e + 1) * FF)
                pool.wait_ge(w1_loaded[e % 2], 16 * (e // 2 + 1))
                g_.tensor_copy(w1_part[:, 0, units], w1_raw[:, e % 2, :]).then_inc(w1_high, 1)
                pool.wait_ge(w1_high, e + 1)
                g_.tensor_tensor(w1_part[:, 1, units], w1_raw[:, e % 2, :], w1_part[:, 0, units].bitcast(F32),
                                 ALU.subtract).then_inc(w1_ready, 1)

            def residual_base(g):
                par = g % 2
                if g == 0:
                    pool.wait_ge(const_in, 16 * 6)
                pool.wait_ge(xg_loaded[par], 16 * (g // 2 + 1))
                g_.tensor_tensor(xg[:, par, :, :], xg[:, par, :, :],
                                 bout_sb[:, :].unsqueeze(1).to_broadcast([P, GT, D]), ALU.add).then_inc(xb_done, 1)

            def inverse_deviation(g):
                par = g % 2
                pool.wait_ge(ve_ready, g + 1)
                reach(pool, x1_ready, g - 1)
                g_.tensor_tensor(rstd[:, par, :], var_eps[:, par, :], minus_half[:, :], ALU.pow).then_inc(rstd_ready, 1)

            def token_numbers(g):
                ring = g % XR
                if g >= XR:
                    pool.wait_ge(scattered[ring], 16 * GT * (g // XR))
                g_.iota(x1[:, ring, :, D:D + 1].bitcast(I32), pattern=[[P, GT], [0, 1]], base=g * GT * P,
                        channel_multiplier=1).then_inc(number_ready, 1)

            def scatter(g, tiles):
                ring = g % XR
                pool.wait_ge(dest_ready, g + 1)
                pool.wait_ge(x1_ready, g + 1)
                pool.wait_ge(number_ready, g + 1)
                for i in tiles:
                    g_.indirect_dma_start(out=sorted_rows, out_offset=bass.IndirectOffsetOnAxis(ap=dest[:, ring, i:i + 1], axis=0),
                                          in_=x1[:, ring, i, :], in_offset=None).then_inc(scattered[ring], 16)

            def group_step(s):
                if 0 <= s - 2 < G:
                    token_numbers(s - 2)
                    inverse_deviation(s - 2)
                if 0 <= s - 4 < G:
                    scatter(s - 4, range(GT))
                if s < G:
                    residual_base(s)

            last_token = pool.to_reg(B * N - 1)

            def tile_step(s):
                if 0 <= s - 1 < NT:
                    t = s - 1
                    pool.wait_ge(ve3_ready, t + 1)
                    reach(pool, y_ready, t - 1)
                    g_.tensor_tensor(rstd3[:, t % 2, :], ve3[:, t % 2, :], minus_half[:, 0:1], ALU.pow).then_inc(rstd3_ready, 1)
                if s >= 2:
                    t = s - 2
                    pool.wait_ge(y_ready, t + 1)
                    g_.indirect_dma_start(out=out_rows, out_offset=bass.IndirectOffsetOnAxis(ap=xs[:, t % XS, D:D + 1].bitcast(I32), axis=0),
                                          in_=y[:, t % NY, :], in_offset=None, bounds_check=last_token,
                                          oob_is_err=False).then_inc(stored[t % NY], 16)

            for kind, s in ORDER:
                if kind == "group":
                    group_step(s)
                else:
                    tile_step(s)
            for i in range(NY):
                pool.wait_ge(stored[i], 16 * len(range(i, NT, NY)))

        @block.tensor
        def _(pe):
            mm = nc.tensor.matmul
            pe.wait_ge(pool_consts, 1)
            pe.wait_ge(const_in, 16 * 6)
            for i in range(2):
                nc.tensor.transpose(bank[0][:, i * P:(i + 1) * P], wqkv_sb[:, i * D:(i + 1) * D], ident[:, :]).then_inc(w_turned, 1)
            pe.wait_ge(w_turn_kept, 1)
            pe.wait_ge(proj_ready, 1)
            for i in (1, 0):
                mm(bank[1 + i][:, :], wT[:, i, :], proj_diag[:, :, :].rearrange("p h f -> p (h f)"),
                   start=True, stop=True).then_inc(w_feat_pre, 1)
            pe.wait_ge(w_high, 3)
            pe.wait_ge(w_low, 3)

            def turn(t):
                b = t // TB
                pe.wait_ge(x_loaded[(t // GT) % 2], 16 * (b + 1))
                reach(pe, xT_low, t)
                nc.tensor.transpose(xT_bank[:, 0:P], xr[:, (t // GT) % 2, t % GT, :], ident[:, :]).then_inc(x_turned, 1)

            def keys_values(t):
                pe.wait_ge(xT_high, t + 1)
                pe.wait_ge(xT_low, t + 1)
                reach(pe, k_done, t - 2)
                reach(pe, v_ready, t - 2)
                product(pair[t % 3], xT_all[:, :, t * P:(t + 1) * P], wkv_part, kv_spans).then_inc(kv_pre, 1)

            def add_kv(t):
                b = t // TB
                pe.wait_ge(k_done, t + 1)
                pe.wait_ge(v_ready, t + 1)
                if t % TB == 0:
                    reach(pe, kvT_kept, b)
                for a in range(2):
                    for k in range(C):
                        heads = slice(k * CD, (k + 1) * CD)
                        last = mm(kv_bank[heads, a * P:(a + 1) * P], ones_kv[:, :] if a else vals[:, t % VB, heads],
                                  kfeat[:, t % 2, k * P:(k + 1) * P],
                                  start=(t % TB == 0 and a == 0), stop=(t % TB == TB - 1), skip_group_check=True)
                last.then_inc(kv_added, 1)

            def turn_kv(b):
                pe.wait_ge(kvT_kept, b + 1)
                pe.wait_ge(k_done, min((b + 1) * TB + 2, T))
                for a in range(2):
                    last = nc.tensor.transpose(kvT_part[kvT_pair(b)][:, a * P:(a + 1) * P], kvT[:, a * P:(a + 1) * P], ident[:, :])
                last.then_inc(kvT_turned, 1)

            for s in range(-4, T + 3):
                if s > TB and s % TB == 2:
                    turn_kv(s // TB - 1)
                if 0 <= s + 2 < T:
                    keys_values(s + 2)
                if s + 4 < T:
                    turn(s + 4)
                if 0 <= s - 1 < T:
                    add_kv(s - 1)

            def q_chunk(g, k):
                n = g * C + k
                reach(pe, q_done, n - QB + 1)
                product(q_bank[n % QB], wq_part[:, :, k * P:(k + 1) * P], xT_all[:, :, g * 512:(g + 1) * 512],
                        [(slice(0, 512), slice(0, 512))]).then_inc(q_pre, 1)

            def attend(g):
                b = g * GT // TB
                pe.wait_ge(q_done, C * (g + 1))
                pe.wait_ge(kv_kept, B)
                reach(pe, attnT_ready, g)
                for a in range(2):
                    for k in range(C):
                        heads = slice(k * CD, (k + 1) * CD)
                        at = (b * 2 + a) * D + k * CD
                        last = mm((den_bank, num_bank)[a == 0][heads, :], kv_diag[:, at:at + CD], qfeat[:, g % 2, k, :],
                                  start=True, stop=True, skip_group_check=True)
                last.then_inc(attn_pre, 1)

            def project(g):
                pe.wait_ge(attnT_ready, g + 1)
                reach(pe, res_ready, g)
                for i in range(GT):
                    last = mm(o_bank[:, i * P:(i + 1) * P], attnT[:, g % 2, i * P:(i + 1) * P], wout_sb[:, :],
                              start=True, stop=True)
                last.then_inc(out_pre, 1)

            def turn_x1(g):
                pe.wait_ge(x1_ready, g + 1)
                reach(pe, x1T_ready, g)
                for i in range(GT):
                    last = nc.tensor.transpose(t2_bank[:, i * P:(i + 1) * P], x1[:, g % XR, i, 0:D], ident[:, :])
                last.then_inc(x1_turned, 1)

            def scores(g):
                pe.wait_ge(x1T_ready, g + 1)
                reach(pe, next_ready, g)
                for i in range(GT):
                    last = mm(s_bank[:, i * E:(i + 1) * E], x1T[:, g % 2, i * P:(i + 1) * P], wr_sb[:, :],
                              start=True, stop=True)
                last.then_inc(score_pre, 1)

            def ranks(g):
                pe.wait_ge(onehot_ready, g + 1)
                slots = s_bank[:, 64:64 + (GT + 1) * E]
                mm(slots, before[:, :], onehot[:, :, :].rearrange("p i e -> p (i e)"), start=True, stop=False)
                for i in range(GT):
                    last = mm(s_bank[:, 64 + (i + 1) * E:64 + (GT + 1) * E], ones_bf[:, :],
                              onehot[:, i:i + 1, :].to_broadcast([P, GT - i, E]), start=False, stop=(i == GT - 1))
                last.then_inc(rank_pre, 1)

            def group_step(s):
                if s < G:
                    q_chunk(s, 0)
                    q_chunk(s, 1)
                if 0 <= s - 4 < G:
                    ranks(s - 4)
                if 0 <= s - 3 < G:
                    turn_x1(s - 3)
                if s < G:
                    q_chunk(s, 2)
                if 0 <= s - 2 < G:
                    project(s - 2)
                if 0 <= s - 1 < G:
                    attend(s - 1)
                if 0 <= s - 3 < G:
                    scores(s - 3)
                if s < G:
                    q_chunk(s, 3)

            w_at = {}

            def weights_of(t):
                w_at[t] = offset(pe, ENG.PE, w_tab, t, (E - 1) * FF)
                if t == 0:
                    pe.wait_ge(ffn_in, 16 * 3)
                    pe.wait_ge(w1_ready, E)
                    pe.wait_ge(w1_high, E)

            def turn(t):
                pe.wait_ge(xs_loaded[t % XS], 16 * (t // XS + 1))
                reach(pe, xsT_low, t)
                nc.tensor.transpose(xs_bank[:, 0:P], xs[:, t % XS, 0:D], ident[:, :]).then_inc(xs_turned, 1)

            def up(t):
                pe.wait_ge(xsT_high, t + 1)
                pe.wait_ge(xsT_low, t + 1)
                reach(pe, hid_ready, t - 1)
                product(h_bank[t % 2], xsT[:, t % 2, :, :], w1_part, [(slice(0, FF), bass.ds(w_at[t], FF))]).then_inc(hid_pre, 1)

            def turn_hidden(t):
                pe.wait_ge(hid_ready, t + 1)
                reach(pe, hT_ready, t)
                if t == 0:
                    pe.wait_ge(attnT_ready, G)
                for k in range(FC):
                    last = nc.tensor.transpose(hT_bank[:, k * P:(k + 1) * P], hid[:, t % 2, k * P:(k + 1) * P], ident[:, :])
                last.then_inc(hid_turned, 1)

            def down(t):
                pe.wait_ge(hT_ready, t + 1)
                reach(pe, yx_ready, t)
                for k in range(FC):
                    last = mm(y_bank[:, 0:D], hT[:, t % 2, k * P:(k + 1) * P], w2_sb[:, bass.ds(w_at[t] + k * D, D)],
                              start=(k == 0), stop=(k == FC - 1))
                last.then_inc(y_pre, 1)

            def tile_step(s):
                if s + 2 < NT:
                    turn(s + 2)
                if 0 <= s + 1 < NT:
                    up(s + 1)
                if s + 2 < NT:
                    weights_of(s + 2)
                if 0 <= s < NT:
                    turn_hidden(s)
                if 0 <= s - 1 < NT:
                    down(s - 1)

            for kind, s in ORDER:
                if kind == "group":
                    group_step(s)
                else:
                    tile_step(s)

        @block.scalar
        def _(act):
            a_ = nc.scalar
            a_.preload_act_table_set("natural_log_exp_and_others")
            act.wait_ge(w_turned, 2)
            a_.copy(wT[:, :, :].rearrange("p a b -> p (a b)"), bank[0][:, 0:2 * P]).then_inc(w_turn_kept, 1)
            a_.copy(wkv_part[:, 0, NF:NF + D], wqkv_sb[:, 2 * D:3 * D]).then_inc(w_high, 1)
            for i in (1, 0):
                act.wait_ge(w_feat_pre, 2 - i)
                a_.copy((wq_part, wkv_part)[i][:, 0, 0:NF], bank[1 + i][:, :]).then_inc(w_high, 1)
            act.wait_ge(pool_consts, 1)

            def keep_xT(t):
                act.wait_ge(x_turned, t + 1)
                a_.copy(xT_all[:, 0, t * P:(t + 1) * P], xT_bank[:, 0:P]).then_inc(xT_high, 1)

            def exp_keys(t):
                act.wait_ge(kv_pre, t + 1)
                reach(act, k_done, t - 2)
                e = kexp[:, t % 3, :].rearrange("p (a f) -> p a f", a=2)
                if t % 2:
                    a_.activation(e, keys[t % 3], ACT.Relu, bias=zero[:, :], scale=-1.0).then_inc(k_neg, 1)
                    act.wait_ge(k_neg, t // 2 + 1)
                    a_.activation(kexp[:, t % 3, :], kexp[:, t % 3, :], ACT.Exp, bias=zero[:, :], scale=-1.0).then_inc(k_exp, 1)
                else:
                    a_.activation(e, keys[t % 3], ACT.Exp).then_inc(k_exp, 1)

            def keep_values(t):
                reach(act, kv_added, t - VB + 1)
                a_.copy(vals[:, t % VB, :], values[t % 3]).then_inc(v_ready, 1)

            def keep_kvT(b):
                act.wait_ge(kv_added, (b + 1) * TB)
                reach(act, kvT_turned, b)
                a_.copy(kvT[:, :], kv_bank[:, 0:2 * P]).then_inc(kvT_kept, 1)

            for s in range(-4, T + 2):
                if 0 <= s + 1 < T:
                    exp_keys(s + 1)
                    keep_values(s + 1)
                if s > TB and s % TB == 1:
                    keep_kvT(s // TB - 1)
                if s + 4 < T:
                    keep_xT(s + 4)

            def exp_q(g, k):
                n = g * C + k
                act.wait_ge(q_pre, n + 1)
                reach(act, q_done, n - QB + 1)
                if k in BY_RELU:
                    a_.activation(qexp[:, n % QB, :], q_bank[n % QB][:, :], ACT.Relu, bias=zero[:, :], scale=-1.0).then_inc(q_neg, 1)
                    act.wait_ge(q_neg, g * len(BY_RELU) + BY_RELU.index(k) + 1)
                    a_.activation(qexp[:, n % QB, :], qexp[:, n % QB, :], ACT.Exp, bias=zero[:, :], scale=-1.0).then_inc(q_exp, 1)
                else:
                    a_.activation(qexp[:, n % QB, :], q_bank[n % QB][:, :], ACT.Exp).then_inc(q_exp, 1)

            def inverse(g):
                act.wait_ge(attn_pre, g + 1)
                reach(act, rden_ready, g - 1)
                a_.activation(den_inv[:, g % 2, :], den_bank[:, :], ACT.Ln, bias=den_eps[:, :]).then_inc(log_ready, 1)
                act.wait_ge(log_ready, g + 1)
                a_.activation(den_inv[:, g % 2, :], den_inv[:, g % 2, :], ACT.Exp, bias=zero[:, :], scale=-1.0).then_inc(inv_ready, 1)

            def layer_norm(g):
                par = g % 2
                act.wait_ge(shift_ready, g + 1)
                act.wait_ge(number_ready, g + 1)
                for i in range(GT):
                    last = a_.activation(x1[:, g % XR, i, 0:D], res[:, par, i, :], ACT.Identity,
                                         bias=shift[:, par, i:i + 1], scale=rstd[:, par, i:i + 1])
                last.then_inc(x1_ready, 1)

            def keep_x1T(g):
                act.wait_ge(x1_turned, g + 1)
                reach(act, score_pre, g - 1)
                a_.copy(x1T[:, g % 2, :], t2_bank[:, :]).then_inc(x1T_ready, 1)

            def group_step(s):
                if s < G:
                    exp_q(s, 0)
                    exp_q(s, 1)
                if 0 <= s - 3 < G:
                    keep_x1T(s - 3)
                if s < G:
                    exp_q(s, 2)
                if 0 <= s - 1 < G:
                    inverse(s - 1)
                if s < G:
                    exp_q(s, 3)
                if 0 <= s - 2 < G:
                    layer_norm(s - 2)

            def tile_step(s):
                if s + 2 < NT:
                    t = s + 2
                    act.wait_ge(xs_turned, t + 1)
                    reach(act, hid_pre, t - 1)
                    a_.copy(xsT[:, t % 2, 0, :], xs_bank[:, 0:P]).then_inc(xsT_high, 1)
                if 0 <= s < NT:
                    t = s
                    act.wait_ge(hid_turned, t + 1)
                    reach(act, y_pre, t - 1)
                    a_.activation(hT[:, t % 2, :], hT_bank[:, :], ACT.Gelu).then_inc(hT_ready, 1)
                if s >= 2:
                    t = s - 2
                    act.wait_ge(shift3_ready, t + 1)
                    if t >= NY:
                        act.wait_ge(stored[t % NY], 16 * (t // NY))
                    a_.activation(y[:, t % NY, :], res3[:, t % 2, :], ACT.Identity, bias=shift3[:, t % 2, :],
                                  scale=rstd3[:, t % 2, :]).then_inc(y_ready, 1)

            for kind, s in ORDER:
                if kind == "group":
                    group_step(s)
                else:
                    tile_step(s)

        @block.vector
        def _(dve):
            v = nc.vector
            dve.wait_ge(pool_consts, 1)
            dve.wait_ge(const_in, 16 * 6)
            v.tensor_tensor(proj_diag[:, :, :], proj_sb[:, :].unsqueeze(1).to_broadcast([P, H, F]),
                            head_mask[:, :].unsqueeze(2).to_broadcast([P, H, F]), ALU.mult).then_inc(proj_ready, 1)
            dve.wait_ge(w_high, 1)
            v.tensor_tensor(wkv_part[:, 1, NF:NF + D], wqkv_sb[:, 2 * D:3 * D], wkv_part[:, 0, NF:NF + D].bitcast(F32),
                            ALU.subtract).then_inc(w_low, 1)
            for i in (1, 0):
                dve.wait_ge(w_high, 3 - i)
                part = (wq_part, wkv_part)[i]
                v.tensor_tensor(part[:, 1, 0:NF], bank[1 + i][:, :], part[:, 0, 0:NF].bitcast(F32), ALU.subtract).then_inc(w_low, 1)

            def low_part(t):
                dve.wait_ge(xT_high, t + 1)
                v.tensor_tensor(xT_all[:, 1, t * P:(t + 1) * P], xT_bank[:, 0:P], xT_all[:, 0, t * P:(t + 1) * P].bitcast(F32),
                                ALU.subtract).then_inc(xT_low, 1)

            def features(t):
                e, f, k = [a.rearrange("p (a f) -> p a f", a=2) if a is not keys[t % 3] else a
                           for a in (kexp[:, t % 3, :], kfeat[:, t % 2, :], keys[t % 3])]
                dve.wait_ge(k_exp, t + 1)
                if t % 2 == 0:
                    v.tensor_scalar(kexp[:, t % 3, :], kexp[:, t % 3, :], 1.0, None, ALU.min).then_inc(k_min, 1)
                    dve.wait_ge(k_min, t // 2 + 1)
                if t > TB and t % TB == 4:
                    keep_kv(t // TB - 1)
                reach(dve, kv_added, t - 1)
                dve.wait_ge(v_ready, t + 1)
                if t % 2:
                    v.scalar_tensor_tensor(f, k, 0.0, e, ALU.max, ALU.add).then_inc(k_done, 1)
                else:
                    v.scalar_tensor_tensor(f, k, 1.0, e, ALU.add, ALU.max).then_inc(k_done, 1)

            def keep_kv(b):
                dve.wait_ge(kvT_turned, b + 1)
                v.tensor_tensor(kv_diag[:, b * 2 * D:(b + 1) * 2 * D], kvT_part[kvT_pair(b)], block_mask[:, :],
                                ALU.mult).then_inc(kv_kept, 1)

            for s in range(-4, T):
                if s >= 0:
                    features(s)
                if s + 4 < T:
                    low_part(s + 4)
            keep_kv(B - 1)

            def q_features(g, k):
                n = g * C + k
                dve.wait_ge(q_exp, n + 1)
                reach(dve, attn_pre, g - 1)
                if k in BY_RELU:
                    v.scalar_tensor_tensor(qfeat[:, g % 2, k, :], q_bank[n % QB][:, :], 0.0, qexp[:, n % QB, :],
                                           ALU.max, ALU.add).then_inc(q_done, 1)
                else:
                    v.tensor_scalar(qexp[:, n % QB, :], qexp[:, n % QB, :], 1.0, None, ALU.min).then_inc(q_min, 1)
                    dve.wait_ge(q_min, g * (C - len(BY_RELU)) + k // 2 + 1)
                    v.scalar_tensor_tensor(qfeat[:, g % 2, k, :], q_bank[n % QB][:, :], 1.0, qexp[:, n % QB, :],
                                           ALU.add, ALU.max).then_inc(q_done, 1)

            def normalise_attn(g):
                dve.wait_ge(inv_ready, g + 1)
                v.scalar_tensor_tensor(newton[:, :], den_bank[:, :], DEN_EPS, den_inv[:, g % 2, :],
                                       ALU.add, ALU.mult).then_inc(newton_ready, 1)
                dve.wait_ge(newton_ready, g + 1)
                v.scalar_tensor_tensor(newton[:, :], newton[:, :], 2.0, den_inv[:, g % 2, :],
                                       ALU.subtract, ALU.mult).then_inc(rden_ready, 1)
                dve.wait_ge(rden_ready, g + 1)
                reach(dve, out_pre, g - 1)
                v.scalar_tensor_tensor(attnT[:, g % 2, :], num_bank[:, :], -1.0, newton[:, :],
                                       ALU.mult, ALU.mult).then_inc(attnT_ready, 1)

            def residual(g):
                par = g % 2
                dve.wait_ge(out_pre, g + 1)
                dve.wait_ge(xb_done, g + 1)
                reach(dve, x1_ready, g - 1)
                v.tensor_tensor(res[:, par, :, :], o_bank[:, :].rearrange("p (i d) -> p i d", i=GT), xg[:, par, :, :],
                                ALU.add).then_inc(res_ready, 1)
                dve.wait_ge(res_ready, g + 1)
                for i in range(GT):
                    last = v.bn_stats(stats[:, i, :], res[:, par, i, :])
                last.then_inc(stats_ready, 1)
                dve.wait_ge(stats_ready, g + 1)
                for i in range(GT):
                    last = v.bn_aggr(mean_var[:, par, i, :], stats[:, i, :])
                last.then_inc(mv_ready, 1)
                dve.wait_ge(mv_ready, g + 1)
                v.tensor_scalar(var_eps[:, par, :], mean_var[:, par, :, 1], LN_EPS, None, ALU.add).then_inc(ve_ready, 1)

            def shift_of(g):
                par = g % 2
                dve.wait_ge(rstd_ready, g + 1)
                reach(dve, x1_ready, g - 1)
                v.scalar_tensor_tensor(shift[:, par, :], mean_var[:, par, :, 0], -1.0, rstd[:, par, :],
                                       ALU.mult, ALU.mult).then_inc(shift_ready, 1)

            def route(g):
                dve.wait_ge(score_pre, g + 1)
                v.tensor_tensor(score[:, :, :], s_bank[:, 0:GT * E].rearrange("p (i e) -> p i e", e=E),
                                br_sb[:, :].unsqueeze(1).to_broadcast([P, GT, E]), ALU.add).then_inc(score_ready, 1)
                dve.wait_ge(score_ready, g + 1)
                for i in range(GT):
                    last = v.max(top[:, i, :], score[:, i, :])
                last.then_inc(top_ready, 1)
                dve.wait_ge(top_ready, g + 1)
                for i in range(GT):
                    last = v.max_index(top_at[:, i, :], top[:, i, :], score[:, i, :])
                last.then_inc(top_at_ready, 1)
                dve.wait_ge(top_at_ready, g + 1)
                v.tensor_tensor(onehot[:, 0:GT, :], expert_no[:, :].unsqueeze(1).to_broadcast([P, GT, E]),
                                top_at[:, :, 0:1].to_broadcast([P, GT, E]), ALU.is_equal).then_inc(onehot_ready, 1)

            def rows(g):
                ring = g % XR
                dve.wait_ge(rank_pre, g + 1)
                if g:
                    dve.wait_ge(next_ready, g)
                slots = s_bank[:, 64:64 + (GT + 1) * E].rearrange("p (i e) -> p i e", e=E)
                v.tensor_tensor(row_of[:, :, :], slots[:, 0:GT, :], next_row[:, :].unsqueeze(1).to_broadcast([P, GT, E]),
                                ALU.add).then_inc(row_ready, 1)
                dve.wait_ge(row_ready, g + 1)
                v.tensor_tensor(next_row[:, :], slots[:, GT, :], next_row[:, :], ALU.add).then_inc(next_ready, 1)
                v.tensor_tensor(row_pick[:, :, :], row_of[:, :, :], onehot[:, 0:GT, :], ALU.mult).then_inc(pick_ready, 1)
                dve.wait_ge(pick_ready, g + 1)
                if g >= XR:
                    dve.wait_ge(scattered[ring], 16 * GT * (g // XR))
                with nc.allow_low_precision(reason="row numbers are exact integers"):
                    v.tensor_reduce(dest[:, ring, :], row_pick[:, :, :], AX.X, ALU.add).then_inc(dest_ready, 1)

            def group_step(s):
                if 0 <= s - 2 < G:
                    normalise_attn(s - 2)
                if s < G:
                    q_features(s, 0)
                    q_features(s, 1)
                    q_features(s, 2)
                if 0 <= s - 2 < G:
                    residual(s - 2)
                if 0 <= s - 4 < G:
                    rows(s - 4)
                if 0 <= s - 2 < G:
                    shift_of(s - 2)
                if 0 <= s - 3 < G:
                    route(s - 3)
                if s < G:
                    q_features(s, 3)

            done = [0]

            def then(ins):
                done[0] += 1
                ins.then_inc(tab_step, 1)
                dve.wait_ge(tab_step, done[0])

            def tiles_of_experts(rounding):
                then(v.tensor_tensor(used[:, :], next_row[0:1, :], region[0:1, :], ALU.subtract))
                then(v.tensor_scalar(used_i[:, :], used[:, :], float(rounding), None, ALU.add))
                then(v.tensor_scalar(tiles_i[:, :], used_i[:, :], P.bit_length() - 1, None, ALU.arith_shift_right))
                then(v.tensor_copy(tiles_f[:, :], tiles_i[:, :]))

            def experts_of_tiles(lo, hi):
                tiles, n = slice(lo, hi), hi - lo
                then(v.tensor_tensor(past[:, tiles, :], tile_no[:, tiles].unsqueeze(2).to_broadcast([1, n, E - 1]),
                                     tiles_end[:, 1:E].unsqueeze(1).to_broadcast([1, n, E - 1]), ALU.is_ge))
                then(v.tensor_reduce(t_expert[:, tiles], past[:, tiles, :], AX.X, ALU.add))
                then(v.tensor_tensor(past_jump[:, tiles, :], past[:, tiles, :],
                                     jump[:, :].unsqueeze(1).to_broadcast([1, n, E - 1]), ALU.mult))
                then(v.tensor_reduce(t_jump[:, tiles], past_jump[:, tiles, :], AX.X, ALU.add))
                then(v.scalar_tensor_tensor(t_row[:, tiles], tile_no[:, tiles], float(P), t_jump[:, tiles], ALU.mult, ALU.add))

            def weights_of_tiles(lo, hi):
                tiles = slice(lo, hi)
                then(v.tensor_scalar(w_tab[:, tiles], t_expert[:, tiles], float(FF), None, ALU.mult))
                then(v.tensor_scalar(b_tab[:, tiles], t_expert[:, tiles], float(FF + D), None, ALU.mult))

            def first_tables():
                dve.wait_ge(next_ready, GA)
                tiles_of_experts(0)
                then(v.tensor_tensor_scan(tiles_end[:, 1:E + 1], ones_e[:, :], tiles_f[:, :], 0.0, ALU.mult, ALU.add))
                then(v.tensor_scalar(tiles_end[:, :], tiles_end[:, :], float(NA), None, ALU.min))
                then(v.tensor_tensor(first_tiles[:, :], tiles_end[:, 1:E + 1], tiles_end[:, 0:E], ALU.subtract))
                then(v.tensor_scalar(jump[:, :], first_tiles[:, 0:E - 1], -float(P), float(CAP), ALU.mult, ALU.add))
                experts_of_tiles(0, NA)
                then(v.tensor_copy(row_tab[:, 0:NA], t_row[:, 0:NA]))
                weights_of_tiles(0, NA)
                assert done[0] == TAB_A

            def last_tables_counts():
                dve.wait_ge(next_ready, G)
                then(v.tensor_copy(pad_at[:, :], next_row[0:1, :]))
                tiles_of_experts(P - 1)
                then(v.tensor_tensor(left[:, :], tiles_f[:, :], first_tiles[:, :], ALU.subtract))
                then(v.tensor_tensor_scan(tiles_end[:, 1:E + 1], ones_e[:, :], left[:, :], float(NA), ALU.mult, ALU.add))
                then(v.tensor_tensor(kept[:, :], tiles_f[:, 0:E - 1], first_tiles[:, 1:E], ALU.subtract))

            def last_tables_experts():
                then(v.tensor_scalar(jump[:, :], kept[:, :], -float(P), float(CAP), ALU.mult, ALU.add))
                then(v.tensor_scalar(base[:, :], first_tiles[:, 0:1], -float(NA), float(P), ALU.add, ALU.mult))
                experts_of_tiles(NA, NT)

            def last_tables_rows():
                then(v.tensor_scalar(row_tab[:, NA:NT], t_row[:, NA:NT], base[:, :], next_row[0:1, E - 1:E], ALU.add, ALU.min))
                weights_of_tiles(NA, NT)
                assert done[0] == TAB_A + TAB_B

            b_at = {}

            def tile_step(s):
                if s + 2 < NT:
                    t = s + 2
                    dve.wait_ge(xsT_high, t + 1)
                    reach(dve, hid_pre, t - 1)
                    v.tensor_tensor(xsT[:, t % 2, 1, :], xs_bank[:, 0:P], xsT[:, t % 2, 0, :].bitcast(F32),
                                    ALU.subtract).then_inc(xsT_low, 1)
                if 0 <= s + 1 < NT:
                    t = s + 1
                    dve.wait_ge(hid_pre, t + 1)
                    reach(dve, hid_turned, t - 1)
                    v.tensor_tensor(hid[:, t % 2, :], h_bank[t % 2][:, :], b12_sb[:, bass.ds(b_at[t], FF)], ALU.add).then_inc(hid_ready, 1)
                if s + 2 < NT:
                    if s + 2 == 0:
                        dve.wait_ge(ffn_in, 16 * 3)
                    b_at[s + 2] = offset(dve, ENG.DVE, b_tab, s + 2, (E - 1) * (FF + D))
                if 0 <= s - 2 < NT:
                    t = s - 2
                    dve.wait_ge(rstd3_ready, t + 1)
                    v.scalar_tensor_tensor(shift3[:, t % 2, :], mv3[:, t % 2, 0:1], -1.0, rstd3[:, t % 2, :],
                                           ALU.mult, ALU.mult).then_inc(shift3_ready, 1)
                if 0 <= s - 1 < NT:
                    t, par = s - 1, (s - 1) % 2
                    dve.wait_ge(y_pre, t + 1)
                    v.tensor_tensor(yx[:, par, :], y_bank[:, 0:D], xs[:, t % XS, 0:D], ALU.add).then_inc(yx_ready, 1)
                    dve.wait_ge(yx_ready, t + 1)
                    reach(dve, y_ready, t - 1)
                    v.tensor_tensor(res3[:, par, :], yx[:, par, :], b12_sb[:, bass.ds(b_at[t] + FF, D)], ALU.add).then_inc(res3_ready, 1)
                    dve.wait_ge(res3_ready, t + 1)
                    v.bn_stats(stats3[:, :], res3[:, par, :]).then_inc(stats3_ready, 1)
                    dve.wait_ge(stats3_ready, t + 1)
                    v.bn_aggr(mv3[:, par, :], stats3[:, :]).then_inc(mv3_ready, 1)
                    dve.wait_ge(mv3_ready, t + 1)
                    v.tensor_scalar(ve3[:, par, :], mv3[:, par, 1:2], LN_EPS, None, ALU.add).then_inc(ve3_ready, 1)

            for kind, s in ORDER:
                if kind == "group":
                    group_step(s)
                    if s == GA + 3:
                        first_tables()
                else:
                    tile_step(s)
                    if s in MORE_TABLES:
                        (last_tables_counts, last_tables_experts, last_tables_rows)[s - MORE_TABLES[0]]()


_INS = ['L0_attn_x', 'L0_attn_w_qkv', 'L0_attn_proj_matrix', 'L0_attn_w_out', 'L0_attn_b_out', 'L0_ffn_wr',
        'L0_ffn_br', 'L0_ffn_w1', 'L0_ffn_b1', 'L0_ffn_w2', 'L0_ffn_b2']
_OUTS = [((4, 1024, 128), 'float32')]


def kernel(**inputs):
    import numpy as _np
    import concourse.bacc as _bacc
    from concourse import mybir as _mybir
    from concourse.bass_utils import run_bass_kernel_spmd as _run

    nc = _bacc.Bacc("TRN2", target_bir_lowering=False, num_devices=1)
    arrays, args = {}, []
    for name in _INS:
        a = _np.ascontiguousarray(inputs[name])
        arrays[f"in_{name}_dram"] = a
        args.append(nc.dram_tensor(f"in_{name}_dram", a.shape, _mybir.dt.from_np(a.dtype), kind="ExternalInput").ap())
    for i, (shape, dtype) in enumerate(_OUTS):
        dt = _mybir.dt.from_np(_np.dtype(dtype))
        args.append(nc.dram_tensor(f"out_{i}_dram", shape, dt, kind="ExternalOutput").ap())
    build(nc, *args)
    r = _run(nc, [arrays], core_ids=[0])
    got = tuple(r.results[0][f"out_{i}_dram"] for i in range(len(_OUTS)))
    return got[0]
```
